# Optimizing a Trainium2 kernel written in Bass

```python
import numpy as np
import jax
import jax.numpy as jnp

def _softmax(x, axis=-1):
    return jax.nn.softmax(x, axis=axis)

def _gelu(x):
    return jax.nn.gelu(x, approximate=True)

def _silu(x):
    return jax.nn.silu(x)

def _sigmoid(x):
    return jax.nn.sigmoid(x)

def _layernorm(x, axis=-1, eps=1e-05):
    m = jnp.mean(x, axis=axis, keepdims=True)
    v = jnp.var(x, axis=axis, keepdims=True)
    return (x - m) / jnp.sqrt(v + eps)

def _scatter_add(tgt, idx, src, axis=0):
    return tgt.at[idx].add(src)

def _segment_sum(src, seg, n):
    return jax.ops.segment_sum(src, seg, n)
kernel_name = 'mk_gnn_preln_d2_gnn_r8_443d4d'

def setup_inputs(seed: int=0):
    np.random.seed(seed)
    _w = jnp.asarray

    def _rec_inputs():
        import jax
        import jax.numpy as jnp
        _gk = jax.random.key(seed)
        x = -0.0001126 + 1 * jax.random.normal(jax.random.fold_in(_gk, 1), (6250, 256), jnp.float32)
        _s = jax.random.randint(jax.random.fold_in(_gk, 2), (50000,), 0, 6250, jnp.int32)
        _d = jax.random.randint(jax.random.fold_in(_gk, 3), (50000,), 0, 6250, jnp.int32)
        _loop = jnp.arange(6250, dtype=jnp.int32)
        src = jnp.concatenate([_s, _d, _loop])
        dst = jnp.concatenate([_d, _s, _loop])
        _o = jnp.argsort(dst, stable=True)
        src = src[_o]
        dst = dst[_o]
        edge_attr_4 = 0.00117183 + 1.0004 * jax.random.normal(jax.random.fold_in(_gk, 12), (106250, 4), jnp.float32)
        edge_attr_8 = -0.000615933 + 0.999959 * jax.random.normal(jax.random.fold_in(_gk, 13), (106250, 8), jnp.float32)
        node_vec1 = jax.random.uniform(jax.random.fold_in(_gk, 15), (6250, 1), jnp.float32, 0.0, 1)
        return (x, src, dst, edge_attr_4, edge_attr_8, node_vec1)
    x, src, dst, edge_attr_4, edge_attr_8, node_vec1 = _rec_inputs()

    def _L0_gnn_setup():
        import jax, jax.numpy as jnp
        import numpy as np
        import math
        N = 3750
        E = 75000
        MUL = 64
        NES = 8
        FCN = 64
        NUM_NEIGHBORS = 20.0
        SILU_NORM = 1.679
        INV_SQRT3 = 1.0 / math.sqrt(3.0)

        def _split(x):
            return (x[:, :MUL], x[:, MUL:].reshape(-1, MUL, 3))
        key = jax.random.key(seed)
        ks = jax.random.split(key, 16)
        inp = {'node_input': jax.random.normal(ks[0], (N, 4 * MUL), jnp.float32), 'node_attr': jnp.ones((N, 1), jnp.float32), 'edge_src': jax.random.randint(ks[1], (E,), 0, N), 'edge_dst': jax.random.randint(ks[2], (E,), 0, N), 'edge_attr': jax.random.normal(ks[3], (E, 4), jnp.float32), 'edge_scalars': jax.random.normal(ks[4], (E, NES), jnp.float32), 'sc_w0': jax.random.normal(ks[5], (MUL, MUL), jnp.float32), 'sc_w1': jax.random.normal(ks[6], (MUL, MUL), jnp.float32), 'lin1_w0': jax.random.normal(ks[7], (MUL, MUL), jnp.float32), 'lin1_w1': jax.random.normal(ks[8], (MUL, MUL), jnp.float32), 'fc_w1': jax.random.normal(ks[9], (NES, FCN), jnp.float32), 'fc_w2': jax.random.normal(ks[10], (FCN, 4 * MUL), jnp.float32), 'lin2_w00': jax.random.normal(ks[11], (MUL, MUL), jnp.float32), 'lin2_w01': jax.random.normal(ks[12], (MUL, MUL), jnp.float32), 'lin2_w10': jax.random.normal(ks[13], (MUL, MUL), jnp.float32), 'lin2_w11': jax.random.normal(ks[14], (MUL, MUL), jnp.float32)}
        return inp
    _L0_gnn_all = _L0_gnn_setup()
    _L0_gnn_in = {k: v for k, v in _L0_gnn_all.items() if k in ('sc_w0', 'sc_w1', 'lin1_w0', 'lin1_w1', 'fc_w1', 'fc_w2', 'lin2_w00', 'lin2_w01', 'lin2_w10', 'lin2_w11')}
    del _L0_gnn_all

    def _L1_gnn_setup():
        import jax, jax.numpy as jnp
        import numpy as np
        N = 6250
        E = 100000
        IN_C = 256
        HID = 64
        HEADS = 4
        NEG_SLOPE = 0.2

        def _gat_conv(x, W, att_src, att_dst, b, src, dst):
            n = x.shape[0]
            h = (x @ W).reshape(n, HEADS, HID)
            a_s = jnp.einsum('nhc,hc->nh', h, att_src)
            a_d = jnp.einsum('nhc,hc->nh', h, att_dst)
            e = jax.nn.leaky_relu(a_s[src] + a_d[dst], NEG_SLOPE)
            m = jax.ops.segment_max(e, dst, num_segments=n)
            ex = jnp.exp(e - m[dst])
            denom = jax.ops.segment_sum(ex, dst, num_segments=n)
            alpha = ex / denom[dst]
            msg = h[src] * alpha[:, :, None]
            out = jax.ops.segment_sum(msg, dst, num_segments=n)
            return out.reshape(n, HEADS * HID) + b
        key = jax.random.key(seed)
        ks = jax.random.split(key, 12)
        x = jax.random.normal(ks[0], (N, IN_C), dtype=jnp.float32)
        edge_index = jax.random.randint(ks[1], (2, E), 0, N, dtype=jnp.int64)
        s1 = 1.0 / np.sqrt(IN_C)
        W1 = jax.random.normal(ks[2], (IN_C, HEADS * HID), dtype=jnp.float32) * s1
        att_src1 = jax.random.normal(ks[3], (HEADS, HID), dtype=jnp.float32) * 0.1
        att_dst1 = jax.random.normal(ks[4], (HEADS, HID), dtype=jnp.float32) * 0.1
        b1 = jnp.zeros((HEADS * HID,), dtype=jnp.float32)
        s2 = 1.0 / np.sqrt(HEADS * HID)
        W2 = jax.random.normal(ks[5], (HEADS * HID, HEADS * HID), dtype=jnp.float32) * s2
        att_src2 = jax.random.normal(ks[6], (HEADS, HID), dtype=jnp.float32) * 0.1
        att_dst2 = jax.random.normal(ks[7], (HEADS, HID), dtype=jnp.float32) * 0.1
        b2 = jnp.zeros((HEADS * HID,), dtype=jnp.float32)
        return {'x': x, 'edge_index': edge_index, 'W1': W1, 'att_src1': att_src1, 'att_dst1': att_dst1, 'b1': b1, 'W2': W2, 'att_src2': att_src2, 'att_dst2': att_dst2, 'b2': b2}
    _L1_gnn_all = _L1_gnn_setup()
    _L1_gnn_in = {k: v for k, v in _L1_gnn_all.items() if k in ('W1', 'att_src1', 'att_dst1', 'b1', 'W2', 'att_src2', 'att_dst2', 'b2')}
    del _L1_gnn_all
    return {'x': x, 'src': src, 'dst': dst, 'edge_attr_4': edge_attr_4, 'edge_attr_8': edge_attr_8, 'node_vec1': node_vec1, 'L0_gnn_sc_w0': _L0_gnn_in['sc_w0'], 'L0_gnn_sc_w1': _L0_gnn_in['sc_w1'], 'L0_gnn_lin1_w0': _L0_gnn_in['lin1_w0'], 'L0_gnn_lin1_w1': _L0_gnn_in['lin1_w1'], 'L0_gnn_fc_w1': _L0_gnn_in['fc_w1'], 'L0_gnn_fc_w2': _L0_gnn_in['fc_w2'], 'L0_gnn_lin2_w00': _L0_gnn_in['lin2_w00'], 'L0_gnn_lin2_w01': _L0_gnn_in['lin2_w01'], 'L0_gnn_lin2_w10': _L0_gnn_in['lin2_w10'], 'L0_gnn_lin2_w11': _L0_gnn_in['lin2_w11'], 'L1_gnn_W1': _L1_gnn_in['W1'], 'L1_gnn_att_src1': _L1_gnn_in['att_src1'], 'L1_gnn_att_dst1': _L1_gnn_in['att_dst1'], 'L1_gnn_b1': _L1_gnn_in['b1'], 'L1_gnn_W2': _L1_gnn_in['W2'], 'L1_gnn_att_src2': _L1_gnn_in['att_src2'], 'L1_gnn_att_dst2': _L1_gnn_in['att_dst2'], 'L1_gnn_b2': _L1_gnn_in['b2']}

def reference(x, src, dst, edge_attr_4, edge_attr_8, node_vec1, L0_gnn_sc_w0, L0_gnn_sc_w1, L0_gnn_lin1_w0, L0_gnn_lin1_w1, L0_gnn_fc_w1, L0_gnn_fc_w2, L0_gnn_lin2_w00, L0_gnn_lin2_w01, L0_gnn_lin2_w10, L0_gnn_lin2_w11, L1_gnn_W1, L1_gnn_att_src1, L1_gnn_att_dst1, L1_gnn_b1, L1_gnn_W2, L1_gnn_att_src2, L1_gnn_att_dst2, L1_gnn_b2):
    import jax
    import jax.numpy as jnp

    def _L0_gnn_ref(node_input, node_attr, edge_src, edge_dst, edge_attr, edge_scalars, sc_w0, sc_w1, lin1_w0, lin1_w1, fc_w1, fc_w2, lin2_w00, lin2_w01, lin2_w10, lin2_w11):
        import jax, jax.numpy as jnp
        import numpy as np
        import math
        N = 3750
        E = 75000
        MUL = 64
        NES = 8
        FCN = 64
        NUM_NEIGHBORS = 20.0
        SILU_NORM = 1.679
        INV_SQRT3 = 1.0 / math.sqrt(3.0)

        def _split(x):
            return (x[:, :MUL], x[:, MUL:].reshape(-1, MUL, 3))
        n = node_input.shape[0]
        inv_mul = 1.0 / math.sqrt(MUL)
        x0, x1 = _split(node_input)
        a = node_attr
        s0 = x0 @ sc_w0 * a * inv_mul
        s1 = jnp.einsum('nuc,uv->nvc', x1, sc_w1) * a[:, :, None] * inv_mul
        y0 = x0 @ lin1_w0 * a * inv_mul
        y1 = jnp.einsum('nuc,uv->nvc', x1, lin1_w1) * a[:, :, None] * inv_mul
        h = jax.nn.silu(edge_scalars @ fc_w1 * (1.0 / math.sqrt(NES))) * SILU_NORM
        w = h @ fc_w2 * (1.0 / math.sqrt(FCN))
        w_a, w_b, w_c, w_d = (w[:, :MUL], w[:, MUL:2 * MUL], w[:, 2 * MUL:3 * MUL], w[:, 3 * MUL:])
        xg0 = y0[edge_src]
        xg1 = y1[edge_src]
        ea0 = edge_attr[:, :1]
        ea1 = edge_attr[:, 1:4]
        mid0 = w_a * xg0 * ea0
        mid1 = w_b * jnp.einsum('euc,ec->eu', xg1, ea1) * INV_SQRT3
        mid2 = (w_c * xg0)[:, :, None] * ea1[:, None, :]
        mid3 = (w_d * ea0)[:, :, None] * xg1
        mids = jnp.concatenate([mid0, mid1, mid2.reshape(-1, 3 * MUL), mid3.reshape(-1, 3 * MUL)], axis=1)
        agg = jax.ops.segment_sum(mids, edge_dst, num_segments=n)
        agg = agg * (1.0 / math.sqrt(NUM_NEIGHBORS))
        z0a = agg[:, :MUL]
        z0b = agg[:, MUL:2 * MUL]
        z1a = agg[:, 2 * MUL:5 * MUL].reshape(n, MUL, 3)
        z1b = agg[:, 5 * MUL:].reshape(n, MUL, 3)
        inv2 = 1.0 / math.sqrt(2 * MUL)
        o0 = (z0a @ lin2_w00 + z0b @ lin2_w01) * a * inv2
        o1 = (jnp.einsum('nuc,uv->nvc', z1a, lin2_w10) + jnp.einsum('nuc,uv->nvc', z1b, lin2_w11)) * a[:, :, None] * inv2
        c_s = math.sin(math.pi / 8.0)
        c_x = math.cos(math.pi / 8.0)
        out0 = c_s * s0 + c_x * o0
        out1 = c_s * s1 + c_x * o1
        return jnp.concatenate([out0, out1.reshape(n, 3 * MUL)], axis=1)

    def _L1_gnn_ref(x, edge_index, W1, att_src1, att_dst1, b1, W2, att_src2, att_dst2, b2):
        import jax, jax.numpy as jnp
        import numpy as np
        N = 6250
        E = 100000
        IN_C = 256
        HID = 64
        HEADS = 4
        NEG_SLOPE = 0.2

        def _gat_conv(x, W, att_src, att_dst, b, src, dst):
            n = x.shape[0]
            h = (x @ W).reshape(n, HEADS, HID)
            a_s = jnp.einsum('nhc,hc->nh', h, att_src)
            a_d = jnp.einsum('nhc,hc->nh', h, att_dst)
            e = jax.nn.leaky_relu(a_s[src] + a_d[dst], NEG_SLOPE)
            m = jax.ops.segment_max(e, dst, num_segments=n)
            ex = jnp.exp(e - m[dst])
            denom = jax.ops.segment_sum(ex, dst, num_segments=n)
            alpha = ex / denom[dst]
            msg = h[src] * alpha[:, :, None]
            out = jax.ops.segment_sum(msg, dst, num_segments=n)
            return out.reshape(n, HEADS * HID) + b
        loop = jnp.arange(N, dtype=edge_index.dtype)
        src = jnp.concatenate([edge_index[0], loop])
        dst = jnp.concatenate([edge_index[1], loop])
        h = _gat_conv(x, W1, att_src1, att_dst1, b1, src, dst)
        h = jax.nn.elu(h)
        h = _gat_conv(h, W2, att_src2, att_dst2, b2, src, dst)
        h = jax.nn.elu(h)
        return h
    edge_index = jnp.stack([src, dst])
    h = jnp.maximum(_layernorm(x, axis=-1), 0.0)
    x = x + _L0_gnn_ref(h, node_vec1, src, dst, edge_attr_4, edge_attr_8, L0_gnn_sc_w0, L0_gnn_sc_w1, L0_gnn_lin1_w0, L0_gnn_lin1_w1, L0_gnn_fc_w1, L0_gnn_fc_w2, L0_gnn_lin2_w00, L0_gnn_lin2_w01, L0_gnn_lin2_w10, L0_gnn_lin2_w11)
    h = jnp.maximum(_layernorm(x, axis=-1), 0.0)
    x = x + _L1_gnn_ref(h, edge_index, L1_gnn_W1, L1_gnn_att_src1, L1_gnn_att_dst1, L1_gnn_b1, L1_gnn_W2, L1_gnn_att_src2, L1_gnn_att_dst2, L1_gnn_b2)
    return x

_drawn_inputs = setup_inputs


def setup_inputs(seed=0):
    import zlib

    import numpy as np

    out = dict(_drawn_inputs(seed))
    spreads = {'L1_gnn_b1': (0.0, 0.1), 'L1_gnn_b2': (0.0, 0.1)}
    factors = {'L1_gnn_att_src1': 2.81,
     'L1_gnn_att_dst1': 8.0,
     'L1_gnn_att_src2': 8.0,
     'L1_gnn_att_dst2': 29.743}
    for name, (base, spread) in spreads.items():
        noise = np.random.default_rng([zlib.crc32(name.encode()), seed]).standard_normal(out[name].shape)
        drawn = base * np.exp(spread * noise) if base else spread * noise
        out[name] = jnp.asarray(drawn.astype(out[name].dtype))
    for name, factor in factors.items():
        out[name] = (out[name] * factor).astype(out[name].dtype)
    return out
```

```python
import math
from contextlib import ExitStack

import concourse.bass as bass
from concourse import mybir

F32 = mybir.dt.float32
I32 = mybir.dt.int32
BF16 = mybir.dt.bfloat16
ALU = mybir.AluOpType
ACT = mybir.ActivationFunctionType
AX = mybir.AxisListType

P = 128
NODES, EDGES, FEAT = 6250, 106250, 256
MUL, HEADS, HID = 64, 4, 64
BLOCKS = -(-NODES // P)
TILES = -(-EDGES // P)
PAIRS = -(-TILES // 2)
STEPS = PAIRS + BLOCKS - 1
SLOTS = 2 * STEPS
CHUNKS = -(-TILES // P)
ROWS = CHUNKS * P
SLOT_CHUNKS = -(-SLOTS // P)
SLOT_COLS = SLOT_CHUNKS * P
GROUP = 16
GROUPS = SLOTS // GROUP
ROW = HEADS * (HID + 1)
GATHERED = 256
LOOKED_UP = 16
RING = 8
BIG = 1e30
assert SLOTS % (2 * GROUP) == 0 and TILES < ROWS

IN_SCALE = 1.0 / math.sqrt(MUL)
AGG_SCALE = (1.679 / math.sqrt(64)) / math.sqrt(20.0) / math.sqrt(2 * MUL) * math.cos(math.pi / 8.0)
SELF_SCALE = math.sin(math.pi / 8.0)


def run_tiles(eng, n, unroll, body):
    for k in range(min(unroll, n)):
        body(k, k)
    if n // unroll > 1:
        with eng.Fori(1, n // unroll) as i:
            for u in range(unroll):
                body(i * unroll + u, u)
    for k in range(max(unroll, n // unroll * unroll), n):
        body(k, k % unroll)


def peeled(k, unroll):
    return isinstance(k, int) and k < unroll


class Chain:

    def __init__(self, eng, sem):
        self.eng, self.sem, self.n = eng, sem, 0

    def __call__(self, ins):
        self.n += 1
        ins.then_inc(self.sem, 1)
        self.eng.wait_ge(self.sem, self.n)


def build(nc, a, out):
    ctx = ExitStack()
    with ctx:
        names = {}

        def sb(name, shape, dt=F32):
            return ctx.enter_context(nc.sbuf_tensor(name, shape, dt))

        def sem(name):
            names[name] = names.get(name, 0) + 1
            held = s.phase.enter_context(nc.semaphore(f"{name}_{names[name]}"))
            s.phase_sems.append(held)
            return held

        def dram(name, shape, dt=F32):
            return nc.dram_tensor(name, shape, dt, kind="Internal").ap()

        class S:
            pass

        s = S()
        s.sent = {}

        def swdge(name, n, counts):
            if name not in s.sent:
                s.sent[name] = [[ctx.enter_context(nc.semaphore(f"{name}{i}")), 0] for i in range(n)]
            before = [(x[0], x[1]) for x in s.sent[name]]
            for x, c in zip(s.sent[name], counts):
                x[1] += c
            return before
        s.swdge = swdge
        s.passed = ctx.enter_context(nc.semaphore("waits_passed"))
        s.sb, s.sem, s.dram = sb, sem, dram
        s.y_rows = dram("y_rows", (BLOCKS * P, FEAT))
        s.res_rows = dram("res_rows", (BLOCKS * P, FEAT))
        s.h_rows = dram("h_rows", (BLOCKS * P, ROW))
        s.as_rows = dram("as_rows", (BLOCKS * P, HEADS))
        s.max_rows = dram("max_rows", (ROWS * P, HEADS))
        s.fill_rows = dram("fill_rows", (ROWS * P, 2 * HEADS))
        s.ex_rows = dram("ex_rows", (ROWS, HEADS * P))
        s.lo_rows = dram("lo_rows", (ROWS, P), BF16)
        s.first_line = dram("first_line", (BLOCKS * P + 1, 1))
        s.block_line = dram("block_line", (SLOT_COLS, 1), I32)
        s.ident = sb("ident", [P, P])
        s.ones = sb("ones", [P, P])
        s.iota = sb("iota", [P, P])
        s.acol = sb("acol", [P, BLOCKS])
        s.src_t = sb("src_t", [P, ROWS], I32)
        s.src_x = sb("src_x", [P, SLOT_COLS], I32)
        s.dst_x = sb("dst_x", [P, SLOT_COLS])
        s.edge_x = sb("edge_x", [P, 4, SLOT_COLS])
        s.blk = sb("blk", [1, SLOT_COLS], I32)
        s.idx8 = sb("idx8", [P, GROUPS], I32)
        s.t_slot = sb("t_slot", [P, SLOT_CHUNKS], I32)
        s.keep = sb("keep", [P, ROWS])
        s.dmax = sb("dmax", [P, ROWS])
        s.pre = sb("pre", [P, ROWS])
        s.npre = sb("npre", [P, ROWS])
        s.keep_r = sb("keep_r", [8, ROWS])
        s.dmax_r = sb("dmax_r", [8, ROWS])
        s.first_i = sb("first_i", [P, BLOCKS], I32)
        s.last_i = sb("last_i", [P, BLOCKS], I32)
        s.has = sb("has", [P, BLOCKS])
        s.hasb = sb("hasb", [P, BLOCKS])
        s.stat = sb("stat", [P, BLOCKS, 2])
        s.rstd = sb("rstd", [P, BLOCKS])
        s.nmr = sb("nmr", [P, BLOCKS])
        s.asd = sb("asd", [P, BLOCKS, 8])
        s.exself = sb("exself", [P, BLOCKS, HEADS])
        s.node8 = sb("node8", [P, BLOCKS, 8])
        s.z = sb("z", [P, BLOCKS * (FEAT + ROW)])
        s.xr = s.z[:, 0:BLOCKS * FEAT].rearrange("p (k f) -> p k f", f=FEAT)
        s.sums = s.z[:, BLOCKS * FEAT:BLOCKS * (FEAT + ROW)]
        s.work = sb("work", [P, 4096])
        s.ring = sb("ring", [P, RING, ROW])
        s.idx = sb("idx", [P, 2, GROUP], I32)
        s.wk = sb("wk", [P, 2048])
        s.w8 = sb("w8", [P, 8 * P])
        s.w2 = sb("w2", [P, 2 * FEAT])
        s.bias = sb("bias", [P, 2, FEAT])
        s.ps = ctx.enter_context(nc.psum_tensor("ps", [P, 8, 512], F32))
        phase(nc, s, setup, a)
        phase(nc, s, norm_stats, a["x"])
        phase(nc, s, conv_nodes, a)
        phase(nc, s, conv_edges, a)
        phase(nc, s, conv_out, a)
        phase(nc, s, norm_stats)
        for layer in (1, 2):
            phase(nc, s, gat_nodes, a, layer)
            phase(nc, s, gat_scores)
            phase(nc, s, gat_edges)
        phase(nc, s, gat_out, a, out)


def phase(nc, s, program, *args):
    with ExitStack() as s.phase:
        s.phase_sems = []
        program(nc, s, *args)
        with nc.Block() as block:
            @block.gpsimd
            def _(pool):
                for used in s.phase_sems:
                    pool.sem_clear(used)


def setup(nc, s, a):
    loaded, zeroed, made, put, st_blk, got_blk = (s.sem(n) for n in ("loaded", "zeroed", "made", "put", "st_blk", "got_blk"))
    iotas, pl, dv, pe, ac = (s.sem(n) for n in ("iotas", "pool_step", "dve_step", "pe_step", "act_step"))
    st_first, got_next = s.sem("st_first"), s.sem("got_next")
    (g_rows, _), = s.swdge("got_rows", 1, [0])
    (g_sd, _), = s.swdge("got_ints", 1, [0])
    (g_e4, _), = s.swdge("got_floats", 1, [0])
    mm_q, q_ok, mm_last, slot_idx, qi_ok = (s.sem(n) for n in ("mm_q", "q_ok", "mm_last", "slot_idx", "qi_ok"))
    rs_t, rs_sb, re_t, src_ok, tr, ev = (s.sem(n) for n in ("rs_t", "rs_sb", "re_t", "src_ok", "tr", "ev"))
    hs_ok, hs_t, blk_ok, oddb_ok, lb_ok = (s.sem(n) for n in ("hs_ok", "hs_t", "blk_ok", "oddb_ok", "lb_ok"))
    pe_tr = s.sem("pe_tr")
    z = s.z
    o = [0]

    def part(n, dt=F32, shape=None):
        v = z[:, o[0]:o[0] + n]
        o[0] += n
        if dt is not F32:
            v = v.bitcast(dt)
        return v.rearrange(shape[0], **shape[1]) if shape else v

    rows = ("p (c e) -> p c e", dict(e=P))
    d_r = part(ROWS, I32)
    d_p = part(ROWS, I32)
    d1 = part(ROWS)
    cmp = part(58 * 48)
    last_b = part(ROWS)
    last_all = part(ROWS)
    dg = part(BLOCKS * P, I32)
    sd = part(SLOT_CHUNKS * 256, I32, ("p (c e) -> p c e", dict(e=256)))
    e4 = part(SLOT_CHUNKS * 512, F32, ("p (c e) -> p c e", dict(e=512)))
    srcf = part(SLOT_COLS)
    dstf = part(SLOT_COLS)
    zt = part(ROWS * 2)
    sm = part(1300)
    assert o[0] <= BLOCKS * (FEAT + ROW)
    m = [0]

    def small(n, dt=F32):
        v = sm[:, m[0]:m[0] + n]
        m[0] += n
        return v if dt is F32 else v.bitcast(dt)

    io_f, io_p, j_i, jg_i, n_i = small(P, I32), small(1, I32), small(SLOT_CHUNKS, I32), small(GROUPS, I32), small(BLOCKS, I32)
    pi, pf = small(8, I32), small(8)
    lastd, thr, cnt, qb, io48 = small(CHUNKS), small(48), small(48), small(48), small(48)
    jf, bf, tf, negb = (small(SLOT_CHUNKS) for _ in range(4))
    jg, bg, tg = (small(GROUPS) for _ in range(3))
    nf, q, cn, rs, re = (small(BLOCKS) for _ in range(5))
    qi, hs, bi = small(BLOCKS, I32), small(CHUNKS), small(SLOT_CHUNKS, I32)
    hsb = small(CHUNKS * 8)
    tr49 = small(P)
    oddb = s.wk[:, 0:P]
    etile = small(1)
    nxt = small(P)
    lo_ok, src_in = s.sem("lo_ok"), s.sem("src_in")
    src_r, lo_i = s.work[:, 0:ROWS].bitcast(I32), s.work[:, ROWS:2 * ROWS].bitcast(I32)
    lo_b = s.work[:, 2 * ROWS:2 * ROWS + ROWS // 2].bitcast(BF16)

    with nc.Block() as block:
        @block.sync
        def _(sp):
            for dst, src in ((d_r, a["dst_rows"]), (d_p, a["prev_rows"])):
                sp.dma_start(dst.rearrange("p (c e) -> p c e", e=P),
                             src.rearrange("(c p) e -> p c e", p=P)).then_inc(loaded, 16)
            sp.dma_start(s.src_t[:, :], a["src_t"]).then_inc(made, 16)
            sp.dma_start(src_r.rearrange("p (c e) -> p c e", e=P),
                         a["sd_rows"][:, 0:P].rearrange("(c p) e -> p c e", p=P)).then_inc(src_in, 16)
            sp.dma_start(s.acol[:, :], a["a_cols"]).then_inc(made, 16)
            sp.wait_ge(zeroed, 1)
            fill = s.fill_rows.rearrange("(h p r) q -> h p (r q)", p=P, h=4)
            for h in range(4):
                sp.dma_start(fill[h], zt).then_inc(put, 16)
            sp.wait_ge(lo_ok, 1)
            sp.dma_start(s.lo_rows.rearrange("(c p) e -> p c e", p=P), lo_b.rearrange("p (c e) -> p c e", e=P)).then_inc(put, 16)
            sp.wait_ge(blk_ok, 1)
            with nc.allow_non_contiguous_dma(reason="1024 words, once"):
                sp.dma_start(s.block_line.rearrange("(c p) o -> p (c o)", p=P), bi).then_inc(st_blk, 16)
            sp.wait_ge(st_blk, 16)
            sp.dma_start(s.blk[:, :], s.block_line.rearrange("n o -> o n")).then_inc(got_blk, 16)
            sp.wait_ge(rs_sb, 1)
            sp.dma_start(s.first_line[0:BLOCKS * P, :].rearrange("(k p) o -> k (p o)", p=P), tr49[0:BLOCKS, :]).then_inc(st_first, 16)
            sp.dma_start(s.first_line[BLOCKS * P:BLOCKS * P + 1, :], etile[0:1, :]).then_inc(st_first, 16)
            sp.wait_ge(st_first, 32)
            sp.dma_start(nxt[0:BLOCKS, :], s.first_line[1:BLOCKS * P + 1, :].rearrange("(k p) o -> k (p o)", p=P)).then_inc(got_next, 16)
            sp.wait_ge(got_next, 16)
            sp.wait_ge(got_blk, 16)
            sp.wait_ge(made, 32)
            sp.wait_ge(put, 80)

        @block.gpsimd
        def _(pool):
            step = Chain(pool, pl)
            pool.iota(io_f, [[1, P]], base=0, channel_multiplier=0).then_inc(iotas, 1)
            pool.iota(io_p, [[1, 1]], base=0, channel_multiplier=1).then_inc(iotas, 1)
            pool.iota(j_i, [[64, SLOT_CHUNKS]], base=0, channel_multiplier=0).then_inc(iotas, 1)
            pool.iota(jg_i, [[8, GROUPS]], base=0, channel_multiplier=0).then_inc(iotas, 1)
            pool.iota(n_i, [[P, BLOCKS]], base=0, channel_multiplier=1).then_inc(iotas, 1)
            pool.memset(s.ones[:, :], 1.0).then_inc(iotas, 1)
            step(pool.memset(s.ident[:, :], 0.0))
            pool.affine_select(out=s.ident[:, :], in_=s.ident[:, :], compare_op=ALU.not_equal, fill=1.0,
                               base=0, pattern=[[-1, P]], channel_multiplier=1).then_inc(iotas, 1)
            pool.wait_ge(qi_ok, 1)
            for k in range(BLOCKS):
                pool.indirect_dma_start(out=dg[:, k * P:(k + 1) * P], out_offset=None, in_=a["dst_rows"],
                                        in_offset=bass.IndirectOffsetOnAxis(ap=qi[:, k:k + 1], axis=0)).then_inc(g_rows, 16)
            pool.wait_ge(slot_idx, 1)
            for c in range(SLOT_CHUNKS):
                for dst, src, got in ((sd, a["sd_rows"], g_sd), (e4, a["ea4_rows"], g_e4)):
                    pool.indirect_dma_start(out=dst[:, c, :], out_offset=None, in_=src,
                                            in_offset=bass.IndirectOffsetOnAxis(ap=s.t_slot[:, c:c + 1], axis=0)).then_inc(got, 16)

        @block.vector
        def _(dve):
            step = Chain(dve, dv)
            v = nc.vector
            v.memset(zt, 0.0).then_inc(zeroed, 1)
            step(v.memset(etile[0:1, :], float(EDGES)))
            dve.wait_ge(iotas, 7)
            step(v.tensor_copy(s.iota[:, :], io_f))
            for n, (op, by, op2, by2) in enumerate(((ALU.logical_shift_right, 1, None, None), (ALU.bitwise_and, 1, None, None),
                                                    (ALU.logical_shift_right, 4, None, None), (ALU.logical_shift_right, 3, ALU.bitwise_and, 1),
                                                    (ALU.bitwise_and, 7, None, None))):
                if op2 is None:
                    step(v.tensor_scalar(pi[:, n:n + 1], io_p, by, None, op))
                else:
                    step(v.tensor_scalar(pi[:, n:n + 1], io_p, by, by2, op, op2))
            step(v.tensor_copy(pf[:, 0:5], pi[:, 0:5]))
            half, odd, p16, p8odd, p_and7 = (pf[:, n:n + 1] for n in range(5))
            v.tensor_copy(oddb, odd.broadcast_to([P, P])).then_inc(oddb_ok, 1)
            step(v.tensor_copy(nf, n_i))
            dve.wait_ge(src_in, 16)
            step(v.tensor_scalar(lo_i, src_r, P - 1, None, ALU.bitwise_and))
            v.tensor_copy(lo_b, lo_i).then_inc(lo_ok, 1)
            dve.wait_ge(loaded, 32)
            keep3, d13 = (t.rearrange("p (c e) -> p c e", e=P) for t in (s.keep[:, :], d1))
            step(v.tensor_tensor(s.keep[:, :], d_r, d_p, ALU.not_equal))
            step(v.tensor_reduce(hs, keep3, AX.X, ALU.max))
            v.tensor_copy(hsb.rearrange("p (c h) -> p c h", h=8), hs.unsqueeze(2).broadcast_to([P, CHUNKS, 8])).then_inc(hs_ok, 1)
            step(v.tensor_scalar(s.keep[:, :], s.keep[:, :], -1.0, 1.0, ALU.mult, ALU.add))
            step(v.memset(d1, 0.0))
            step(v.tensor_copy(d13[:, :, 0:1], keep3[:, :, 0:1]))
            step(v.memset(keep3[:, :, 0:1], 0.0))
            step(v.tensor_scalar(s.dmax[:, :], s.keep[:, :], -1.0, BIG, ALU.add, ALU.mult))
            step(v.tensor_tensor_scan(s.pre[:, :], s.keep[:, :], d1, 0.0, ALU.mult, ALU.max))
            step(v.tensor_scalar(s.npre[:, :], s.pre[:, :], -1.0, BIG, ALU.add, ALU.mult))
            step(v.tensor_copy(lastd, d_r.rearrange("p (c e) -> p c e", e=P)[:, :, P - 1]))
            v.tensor_copy(last_b.rearrange("p (c e) -> p c e", e=P), lastd.unsqueeze(2).broadcast_to([P, CHUNKS, P])).then_inc(lb_ok, 1)
            step(v.tensor_scalar(thr, s.iota[:, 0:48], 1.0, float(P), ALU.add, ALU.mult))
            c3 = cmp[:, 0:48 * CHUNKS].rearrange("p (b c) -> p b c", c=CHUNKS)
            step(v.tensor_tensor(c3, lastd.unsqueeze(1).broadcast_to([P, 48, CHUNKS]), thr.unsqueeze(2).broadcast_to([P, 48, CHUNKS]), ALU.is_lt))
            v.tensor_reduce(cnt, c3, AX.X, ALU.add).then_inc(q_ok, 1)
            step(v.tensor_scalar(jf, j_i, half, None, ALU.add))
            step(v.tensor_scalar(jg, jg_i, p16, None, ALU.add))
            dve.wait_ge(mm_q, 1)
            step(v.tensor_scalar(qb, s.ps[:, 0, 0:48], float(PAIRS - 1), None, ALU.min))
            step(v.tensor_tensor(qb, qb, s.iota[:, 0:48], ALU.add))
            for n, jv, bv in ((SLOT_CHUNKS, jf, bf), (GROUPS, jg, bg)):
                c3 = cmp[:, 0:n * 48].rearrange("p (j b) -> p j b", b=48)
                step(v.tensor_tensor(c3, qb.unsqueeze(1).broadcast_to([P, n, 48]), jv.unsqueeze(2).broadcast_to([P, n, 48]), ALU.is_lt))
                step(v.tensor_reduce(bv, c3, AX.X, ALU.add))
            v.tensor_copy(bi, bf).then_inc(blk_ok, 1)
            step(v.tensor_scalar(negb, bf, -float(P), None, ALU.mult))
            step(v.tensor_tensor(tf, jf, bf, ALU.subtract))
            step(v.tensor_scalar(tf, tf, 2.0, odd, ALU.mult, ALU.add))
            v.tensor_scalar(s.t_slot[:, :], tf, float(ROWS - 1), None, ALU.min).then_inc(slot_idx, 1)
            step(v.tensor_tensor(tg, jg, bg, ALU.subtract))
            step(v.tensor_scalar(tg, tg, 2.0, p8odd, ALU.mult, ALU.add))
            step(v.tensor_scalar(s.idx8[:, :], tg, 8.0, p_and7, ALU.mult, ALU.add))
            dve.wait_ge(mm_last, 1)
            step(v.tensor_copy(last_all[:, 0:512], s.ps[:, 1, 0:512]))
            step(v.tensor_copy(last_all[:, 512:ROWS], s.ps[:, 2, 0:ROWS - 512]))
            for k in range(BLOCKS):
                step(v.tensor_scalar(d1, last_all, nf[:, k:k + 1], None, ALU.is_lt, ALU.add, accum_out=q[:, k:k + 1]))
            v.tensor_scalar(qi, q, float(ROWS - 1), None, ALU.min).then_inc(qi_ok, 1)
            dve.wait_ge(g_rows, 16 * BLOCKS)
            dg3 = dg.rearrange("p (k e) -> p k e", e=P)
            dgf = dg.bitcast(F32).rearrange("p (k e) -> p k e", e=P)
            step(v.tensor_tensor(dgf, dg3, nf.unsqueeze(2).broadcast_to([P, BLOCKS, P]), ALU.is_lt))
            step(v.tensor_reduce(cn, dgf, AX.X, ALU.add))
            v.scalar_tensor_tensor(rs, q, float(P), cn, ALU.mult, ALU.add).then_inc(src_ok, 1)
            dve.wait_ge(rs_t, 1)
            v.tensor_copy(tr49[0:BLOCKS, :], s.ps[0:BLOCKS, 3, 0:P]).then_inc(rs_sb, 1)
            dve.wait_ge(re_t, 1)
            step(v.tensor_copy(re, s.ps[:, 4, 0:BLOCKS]))
            step(v.tensor_tensor(s.has[:, :], re, rs, ALU.is_gt))
            step(v.tensor_scalar(s.hasb[:, :], s.has[:, :], -1.0, BIG, ALU.add, ALU.mult))
            step(v.tensor_scalar(s.last_i[:, :], re, -1.0, 0.0, ALU.add, ALU.max))
            step(v.tensor_scalar(cn, s.has[:, :], -1.0, -float(1 << 20), ALU.add, ALU.mult))
            step(v.tensor_tensor(s.first_i[:, :], rs, cn, ALU.add))
            dve.wait_ge(hs_t, 1)
            for b, lo, n in ((5, 0, 512), (6, 512, ROWS - 512)):
                step(v.tensor_scalar(s.keep_r[:, lo:lo + n], s.ps[0:8, b, 0:n], -1.0, 1.0, ALU.mult, ALU.add))
            step(v.tensor_scalar(s.dmax_r[:, :], s.keep_r[:, :], -1.0, BIG, ALU.add, ALU.mult))
            dve.wait_ge(g_sd, 16 * SLOT_CHUNKS)
            step(v.tensor_copy(srcf.rearrange("p (c e) -> p c e", e=P), sd[:, :, 0:P]))
            for c in range(SLOT_CHUNKS):
                v.tensor_scalar(dstf[:, c * P:(c + 1) * P], sd[:, c, P:2 * P], negb[:, c:c + 1], None, ALU.add).then_inc(tr, 1)

        @block.tensor
        def _(pe):
            t = nc.tensor
            pe.wait_ge(oddb_ok, 1)
            pe.wait_ge(q_ok, 1)
            t.matmul(s.ps[:, 0, 0:48], oddb, cnt, start=True, stop=True).then_inc(mm_q, 1)
            pe.wait_ge(lb_ok, 1)
            for c in range(CHUNKS):
                last = t.matmul(s.ps[:, 1 + c // 4, c % 4 * P:c % 4 * P + P], last_b[:, c * P:(c + 1) * P], s.ident[:, :], start=True, stop=True)
            last.then_inc(mm_last, 1)
            pe.wait_ge(hs_ok, 1)
            for c in range(CHUNKS):
                last = t.transpose(s.ps[0:8, 5 + c // 4, c % 4 * P:c % 4 * P + P], hsb[:, c * 8:c * 8 + 8], s.ident[:, :])
            last.then_inc(hs_t, 1)
            pe.wait_ge(src_ok, 1)
            t.transpose(s.ps[0:BLOCKS, 3, 0:P], rs, s.ident[:, :]).then_inc(rs_t, 1)
            pe.wait_ge(got_next, 16)
            t.transpose(s.ps[:, 4, 0:BLOCKS], nxt[0:BLOCKS, :], s.ident[0:BLOCKS, 0:BLOCKS]).then_inc(re_t, 1)
            pe.wait_ge(mm_q, 1)
            pe.wait_ge(tr, SLOT_CHUNKS)
            pe.wait_ge(g_e4, 16 * SLOT_CHUNKS)
            pe.wait_ge(dv, 1)
            for c in range(SLOT_CHUNKS):
                if c >= 1:
                    pe.wait_ge(ev, c)
                t.transpose(s.ps[:, 7, 0:P], srcf[:, c * P:(c + 1) * P], s.ident[:, :])
                last = t.transpose(s.ps[:, 7, P:2 * P], dstf[:, c * P:(c + 1) * P], s.ident[:, :])
                last.then_inc(pe_tr, 1)
                for q4 in range(4):
                    last = t.transpose(s.ps[:, 3, q4 * P:(q4 + 1) * P], e4[:, c, q4 * P:(q4 + 1) * P], s.ident[:, :])
                last.then_inc(pe_tr, 1)

        @block.scalar
        def _(act):
            act.wait_ge(rs_sb, 1)
            for c in range(SLOT_CHUNKS):
                act.wait_ge(pe_tr, 2 * c + 2)
                nc.scalar.activation(s.src_x[:, c * P:(c + 1) * P], s.ps[:, 7, 0:P], ACT.Copy)
                nc.scalar.activation(s.dst_x[:, c * P:(c + 1) * P], s.ps[:, 7, P:2 * P], ACT.Copy)
                nc.scalar.activation(s.edge_x[:, :, c * P:(c + 1) * P],
                                     s.ps[:, 3, :].rearrange("p (q e) -> p q e", e=P), ACT.Copy).then_inc(ev, 1)


def norm_stats(nc, s, x=None):
    dv, var_ok, sd_ok, x_ok = (s.sem(n) for n in ("dve_step", "var_ok", "sd_ok", "x_ok"))
    var = s.stat[:, :, 1]
    six = s.wk[:, 0:BLOCKS * 6].rearrange("p (k q) -> p k q", q=6)
    with nc.Block() as block:
        if x is not None:
            @block.sync
            def _(sp):
                sp.dma_start(s.xr, x.rearrange("(k p) f -> p k f", p=P)).then_inc(x_ok, 16)

        @block.vector
        def _(dve):
            step = Chain(dve, dv)
            if x is not None:
                dve.wait_ge(x_ok, 16)
            for k in range(BLOCKS):
                last = nc.vector.bn_stats(six[:, k, :], s.xr[:, k, :])
            step(last)
            for k in range(BLOCKS):
                last = nc.vector.bn_aggr(s.stat[:, k, :], six[:, k, :])
            step(last)
            nc.vector.tensor_scalar(s.rstd[:, :], var, 1e-5, None, ALU.add).then_inc(var_ok, 1)
            dve.wait_ge(sd_ok, 1)
            step(nc.vector.reciprocal(s.rstd[:, :], s.nmr[:, :]))
            nc.vector.scalar_tensor_tensor(s.nmr[:, :], s.stat[:, :, 0], -1.0, s.rstd[:, :], ALU.mult, ALU.mult)

        @block.scalar
        def _(act):
            act.wait_ge(var_ok, 1)
            nc.scalar.activation(s.nmr[:, :], s.rstd[:, :], ACT.Sqrt).then_inc(sd_ok, 1)


def normed(nc, s, dst, k, split):
    kw = dict(bias=s.nmr[:, bass.ds(k, 1)], scale=s.rstd[:, bass.ds(k, 1)])
    row = s.xr[:, bass.ds(k, 1), :].rearrange("p o f -> p (o f)")
    if not split:
        return nc.scalar.activation(dst, row, ACT.Relu, **kw)
    nc.scalar.activation(dst[:, 0:MUL], row[:, 0:MUL], ACT.Relu, **kw)
    return nc.scalar.activation(dst[:, MUL:].rearrange("p (c u) -> p u c", c=3),
                                row[:, MUL:].rearrange("p (u c) -> p u c", c=3), ACT.Relu, **kw)


def project(nc, s, src_of, src_ready, src_used, widths, t_ok, t_sb, mm_ok, mm_used, hT):
    def pe_tile(pe):
        def tile(k, u):
            pe.wait_ge(src_ready, k + 1)
            if not peeled(k, 2):
                pe.wait_ge(t_sb, k - 1)
            for h in range(2):
                last = nc.tensor.transpose(s.ps[:, u, h * P:(h + 1) * P], src_of(u)[:, h * P:(h + 1) * P], s.ident[:, :])
            last.then_inc(t_ok, 1)
            pe.wait_ge(t_sb, k + 1)
            if not peeled(k, 2):
                pe.wait_ge(mm_used, k - 1)
            for out, parts in widths(u):
                for n, (half, w) in enumerate(parts):
                    last = nc.tensor.matmul(out, hT[:, u, half, :], w, start=(n == 0), stop=(n == len(parts) - 1))
            last.then_inc(mm_ok, 1)
        return tile

    def copy_t(dve, k, u):
        dve.wait_ge(t_ok, k + 1)
        if not peeled(k, 2):
            dve.wait_ge(mm_ok, k - 1)
        nc.vector.tensor_copy(hT[:, u, :, :].rearrange("p h n -> p (h n)"), s.ps[:, u, 0:FEAT]).then_inc(t_sb, 1)
    return pe_tile, copy_t


def conv_nodes(nc, s, a):
    wt, wz, hc_ok, t_ok, t_sb, mm_ok, mm_used, y_ok = (s.sem(n) for n in
        ("weights", "weights_zero", "hc_ok", "t_ok", "t_sb", "mm_ok", "mm_used", "y_ok"))
    stored = [s.sem("y_stored") for _ in range(2)]
    dv, sc_ok = s.sem("dve_step"), s.sem("scales")
    wk = s.work
    hc = wk[:, 0:512].rearrange("p (u f) -> p u f", u=2)
    hT = wk[:, 512:1024].rearrange("p (u h n) -> p u h n", u=2, h=2)
    ysb = wk[:, 1024:1536].rearrange("p (u f) -> p u f", u=2)
    ain, aself = wk[:, 1536:1536 + BLOCKS], wk[:, 1600:1600 + BLOCKS]
    res_stored = s.sem("res_stored")
    w = s.wk[:, 0:512].rearrange("p (h f) -> p h f", h=2)
    lo, hi = slice(0, MUL), slice(MUL, P)

    def widths(u):
        return [(s.ps[:, 2 + u, h * 256:(h + 1) * 256], [(h, w[:, h, :])]) for h in range(2)]

    pe_tile, copy_t = project(nc, s, lambda u: hc[:, u, :], hc_ok, None, widths, t_ok, t_sb, mm_ok, mm_used, hT)
    with nc.Block() as block:
        @block.sync
        def _(sp):
            sp.wait_ge(wz, 1)
            for h in range(2):
                for n, (rows, name) in enumerate(((lo, "lin1_w1" if h else "lin1_w0"), (hi, "lin1_w1"),
                                                  (lo, "sc_w1" if h else "sc_w0"), (hi, "sc_w1"))):
                    sp.dma_start(w[rows, h, n * MUL:(n + 1) * MUL], a[name]).then_inc(wt, 16)

            def tile(k, u):
                sp.wait_ge(y_ok, k + 1)
                sp.dma_start(s.y_rows[bass.ds(k * P, P), :], ysb[:, u, :]).then_inc(stored[u], 16)
                sp.wait_ge(mm_used, k + 1)
                sp.dma_start(s.res_rows[bass.ds(k * P, P), :], s.xr[:, bass.ds(k, 1), :].rearrange("p o f -> p (o f)")).then_inc(res_stored, 16)
            run_tiles(sp, BLOCKS, 2, tile)
            sp.wait_ge(res_stored, 16 * BLOCKS)
            for u in range(2):
                sp.wait_ge(stored[u], 16 * ((BLOCKS + 1 - u) // 2))

        @block.scalar
        def _(act):
            def tile(k, u):
                if not peeled(k, 2):
                    act.wait_ge(t_ok, k - 1)
                normed(nc, s, hc[:, u, :], k, True).then_inc(hc_ok, 1)
            run_tiles(act, BLOCKS, 2, tile)

        @block.tensor
        def _(pe):
            pe.wait_ge(wt, 16 * 8)
            run_tiles(pe, BLOCKS, 2, pe_tile(pe))

        @block.vector
        def _(dve):
            step = Chain(dve, dv)
            nc.vector.memset(s.wk[:, 0:512], 0.0).then_inc(wz, 1)
            step(nc.vector.tensor_scalar(ain, s.acol[:, :], IN_SCALE, None, ALU.mult))
            step(nc.vector.tensor_scalar(aself, s.acol[:, :], IN_SCALE * SELF_SCALE, None, ALU.mult))

            def tile(k, u):
                copy_t(dve, k, u)
                dve.wait_ge(mm_ok, k + 1)
                if not peeled(k, 2):
                    dve.wait_ge(stored[u], (k - u) * 8)
                ps = s.ps[:, 2 + u, :]
                nc.vector.tensor_scalar(ysb[:, u, :].rearrange("p (h f) -> p h f", h=2),
                                        ps.rearrange("p (h g f) -> p h g f", h=2, g=2)[:, :, 0, :],
                                        ain[:, bass.ds(k, 1)], None, ALU.mult).then_inc(y_ok, 1)
                row = s.xr[:, bass.ds(k, 1), :].rearrange("p o f -> p (o f)")
                vec = row[:, MUL:].rearrange("p (u c) -> p c u", c=3)
                sc = aself[:, bass.ds(k, 1)]
                nc.vector.scalar_tensor_tensor(row[:, 0:MUL], ps[:, 128:192], sc, row[:, 0:MUL], ALU.mult, ALU.add)
                nc.vector.scalar_tensor_tensor(vec[:, 0, :], ps[:, 192:256], sc, vec[:, 0, :], ALU.mult, ALU.add)
                nc.vector.scalar_tensor_tensor(vec[:, 1:3, :], ps[:, 384:512].rearrange("p (c u) -> p c u", c=2), sc,
                                               vec[:, 1:3, :], ALU.mult, ALU.add).then_inc(mm_used, 1)
            run_tiles(dve, BLOCKS, 2, tile)


def pool_wait(pool, s, sem, value):
    pool.wait_ge(sem, value)
    if not isinstance(value, int):
        pool.sem_inc(s.passed)


def gather_slots(pool, s, table, width, idx_ok, got, msg_ok, extra=None):
    def half(g, u):
        pool_wait(pool, s, idx_ok, g + 1)
        if extra:
            extra(g, u)
        for n in range(GROUP):
            r = n % RING
            if n % 2 == 0 and not (isinstance(g, int) and g == 0 and n < RING):
                pool_wait(pool, s, msg_ok, g * 8 + n // 2 - RING // 2 + 1)
            pool.indirect_dma_start(out=s.ring[:, r, 0:width], out_offset=None, in_=table,
                                    in_offset=bass.IndirectOffsetOnAxis(ap=s.idx[:, u, n:n + 1], axis=0)).then_inc(got[r][0], 16)
    run_tiles(pool, GROUPS, 2, half)


def landed(eng, got, g, n):
    arrived, before = got[n % RING]
    eng.wait_ge(arrived, (g * (GROUP // RING) + n // RING + 1) * 16 + before)


def conv_edges(nc, s, a):
    wt, wz, idx_ok, pre_ok, h_ok, w_ok, msg_ok, sel_ok, agg_ok, zero_ok, z_ok = (s.sem(n) for n in
        ("weights", "weights_zero", "idx_ok", "pre_ok", "h_ok", "w_ok", "msg_ok", "sel_ok", "agg_ok", "zero_ok", "z_ok"))
    eq_ok = s.sem("eq_ok")
    got = s.swdge("ring", RING, [SLOTS // RING * 16] * RING)
    got8 = s.swdge("got8_", 2, [0, 0])
    yg = s.ring[:, :, 0:FEAT]
    e8 = s.sb("e8", [P, 2, P])
    i8 = s.sb("i8", [P, 2, 1], I32)
    h2 = s.sb("h2", [P, 2, 2, P])
    msg = s.work[:, 0:2048].rearrange("p (b k f) -> p b k f", b=2, k=2)
    sel = s.work[:, 2048:4096].rearrange("p (b k c n) -> p b k c n", b=2, k=2, c=4)
    eq = s.sb("eq", [P, 2, 2, P])
    w8 = s.w8[:, :].rearrange("p (q m) -> p q m", q=8)
    ps = s.ps
    tail = (GROUPS - 1) % 2

    with nc.Block() as block:
        @block.sync
        def _(sp):
            sp.wait_ge(wz, 2)
            for n in range(GROUP):
                sp.dma_start(w8[8 * n:8 * n + 8, n // 2, n % 2 * 64:n % 2 * 64 + 64], a["fc_w1"]).then_inc(wt, 16)
            for h in range(2):
                sp.dma_start(s.w2[h * 64:(h + 1) * 64, h * FEAT:(h + 1) * FEAT], a["fc_w2"]).then_inc(wt, 16)

        @block.gpsimd
        def _(pool):
            def scalars(g, u):
                if not peeled(g, 2):
                    pool_wait(pool, s, pre_ok, (g - 1) * 4)
                pool.indirect_dma_start(out=e8[:, u, :], out_offset=None, in_=a["ea8_rows"],
                                        in_offset=bass.IndirectOffsetOnAxis(ap=i8[:, u, :], axis=0)).then_inc(got8[u][0], 16)
            gather_slots(pool, s, s.y_rows, FEAT, idx_ok, got, msg_ok, scalars)

        @block.scalar
        def _(act):
            def stage(g, u):
                if not peeled(g, 2):
                    act.wait_ge(msg_ok, (g - 1) * 8)
                nc.scalar.activation(i8[:, u, :], s.idx8[:, bass.ds(g, 1)], ACT.Copy)
                nc.scalar.activation(s.idx[:, u, :], s.src_x[:, bass.ds(g * GROUP, GROUP)], ACT.Copy).then_inc(idx_ok, 1)

            def silu(g, q):
                n = g * 4 + q
                act.wait_ge(pre_ok, n + 1)
                if not (isinstance(g, int) and g == 0 and q < 2):
                    act.wait_ge(w_ok, 2 * (n - 1))
                nc.scalar.activation(h2[:, q % 2, :, :].rearrange("p a e -> p (a e)"), ps[:, q % 2, 0:2 * P], ACT.Silu,
                                     scale=1.0 / math.sqrt(8.0)).then_inc(h_ok, 1)

            def weights(g, q, b):
                pair = g * 8 + 2 * q + b
                act.wait_ge(eq_ok, pair + 1)
                for k in range(2):
                    slot = bass.ds(pair * 2 + k, 1)
                    for c in range(4):
                        last = nc.scalar.activation(sel[:, b, k, c, :], eq[:, b, k, :], ACT.Copy, scale=s.edge_x[:, c, slot])
                last.then_inc(sel_ok, 1)

            def group(g, u, final=False):
                for q in range(4):
                    if q < 3:
                        silu(g, q + 1)
                    elif not final:
                        silu(g + 1, 0)
                    for b in range(2):
                        weights(g, q, b)
                    if q == 1 and not final:
                        stage(g + 1, 1 - u)
            stage(0, 0)
            silu(0, 0)
            run_tiles(act, GROUPS - 1, 2, group)
            group(GROUPS - 1, tail, True)

        @block.tensor
        def _(pe):
            pe.wait_ge(wt, 16 * (GROUP + 2))

            def first(g, u, q):
                if q == 0:
                    pe.wait_ge(got8[u][0], (g - u) * 8 + 16)
                if not (isinstance(g, int) and g == 0 and q < 2):
                    pe.wait_ge(h_ok, g * 4 + q - 1)
                for b in range(2):
                    last = nc.tensor.matmul(ps[:, q % 2, b * P:(b + 1) * P], w8[:, 2 * q + b, :], e8[:, u, :], start=True, stop=True)
                last.then_inc(pre_ok, 1)

            def second(g, q, b):
                pair = g * 8 + 2 * q + b
                pe.wait_ge(h_ok, g * 4 + q + 1)
                if not (isinstance(g, int) and g == 0 and q == 0):
                    pe.wait_ge(msg_ok, pair - 1)
                nc.tensor.matmul(ps[:, 2 + b, :], h2[:, q % 2, b, :], s.w2[:, :], start=True, stop=True).then_inc(w_ok, 1)

            def collect(g, q, b):
                pair = g * 8 + 2 * q + b
                pe.wait_ge(msg_ok, pair + 1)
                pe.wait_ge(sel_ok, pair + 1)
                if not (isinstance(g, int) and g == 0 and q == 0):
                    pe.wait_ge(z_ok, pair - 1)
                o = ps[:, 4 + b, :]
                for k in range(2):
                    m = msg[:, b, k, :]
                    o4, m4 = (x[:, 256:512].rearrange("p (q f) -> p q f", q=4) for x in (o, m))
                    nc.tensor.matmul(o[:, 0:256], sel[:, b, k, 0, :], m[:, 0:256], start=(k == 0), stop=False, skip_group_check=True)
                    for c in range(3):
                        last = nc.tensor.matmul(o4[:, c:4:3 - c, :], sel[:, b, k, 1 + c, :], m4[:, 0:c + 2:c + 1, :],
                                                start=False, stop=(k == 1 and c == 2), skip_group_check=True)
                last.then_inc(agg_ok, 1)

            def group(g, u, final=False):
                for q in range(4):
                    if q < 3:
                        first(g, u, q + 1)
                    elif not final:
                        first(g + 1, 1 - u, 0)
                    for b in range(2):
                        second(g, q, b)
                        if isinstance(g, int) and g == 0 and q == 0 and b == 0:
                            continue
                        if b:
                            collect(g, q, 0)
                        elif q:
                            collect(g, q - 1, 1)
                        else:
                            collect(g - 1, 3, 1)
            first(0, 0, 0)
            run_tiles(pe, GROUPS - 1, 2, group)
            group(GROUPS - 1, tail, True)
            collect(GROUPS - 1, 3, 1)

        @block.vector
        def _(dve):
            v = nc.vector
            v.memset(s.w8[:, :], 0.0).then_inc(wz, 1)
            v.memset(s.w2[:, :], 0.0).then_inc(wz, 1)
            v.memset(s.z[:, 0:BLOCKS * 512], 0.0).then_inc(zero_ok, 1)
            dve.wait_ge(zero_ok, 1)

            def select(g, q, b):
                pair = g * 8 + 2 * q + b
                if not (isinstance(g, int) and g == 0 and q == 0):
                    dve.wait_ge(agg_ok, pair - 1)
                for k in range(2):
                    last = v.tensor_scalar(eq[:, b, k, :], s.iota[:, :], s.dst_x[:, bass.ds(pair * 2 + k, 1)], None, ALU.is_equal)
                last.then_inc(eq_ok, 1)

            def messages(g, q, b):
                pair = g * 8 + 2 * q + b
                n = 4 * q + 2 * b
                dve.wait_ge(w_ok, pair + 1)
                landed(dve, got, g, n)
                landed(dve, got, g, n + 1)
                w = ps[:, 2 + b, :].rearrange("p (k q f) -> p k q f", k=2, q=4)
                x = yg[:, n % RING:n % RING + 2, :]
                m = msg[:, b, :, :]
                x0 = x[:, :, 0:MUL].unsqueeze(2).broadcast_to([P, 2, 2, MUL])
                v.tensor_tensor(m.rearrange("p k (h f) -> p k h f", h=2)[:, :, :, 0:MUL], w[:, :, 0:3:2, :], x0, ALU.mult)
                x1 = x[:, :, MUL:FEAT].rearrange("p k (c f) -> p k c f", c=3)
                for lo, part in ((64, 3), (320, 1)):
                    last = v.tensor_tensor(m[:, :, lo:lo + 192].rearrange("p k (c f) -> p k c f", c=3),
                                           w[:, :, part, :].unsqueeze(2).broadcast_to([P, 2, 3, MUL]), x1, ALU.mult)
                last.then_inc(msg_ok, 1)

            add = adder(nc, s, dve, s.z, agg_ok, z_ok, 512, lambda b: ps[:, 4 + b, :])

            def group(g, u, final=False):
                for q in range(4):
                    for b in range(2):
                        messages(g, q, b)
                        if not b:
                            select(g, q, 1)
                        elif q < 3:
                            select(g, q + 1, 0)
                        elif not final:
                            select(g + 1, 0, 0)
                        if b:
                            add(g, q, 0)
                        elif q:
                            add(g, q - 1, 1)
                        elif not (isinstance(g, int) and g == 0):
                            add(g - 1, 3, 1)
            select(0, 0, 0)
            run_tiles(dve, GROUPS - 1, 2, group)
            group(GROUPS - 1, tail, True)
            add(GROUPS - 1, 3, 1)


def adder(nc, s, dve, sums, agg_ok, z_ok, width, bank):
    def add(g, q, b):
        pair = g * 8 + 2 * q + b
        block = dve.value_load(s.blk[0:1, bass.ds(pair * 2, 1)], min_val=0, max_val=BLOCKS - 1)
        dve.wait_ge(agg_ok, pair + 1)
        if not (isinstance(g, int) and g == 0 and q == 0 and b == 0):
            dve.wait_ge(z_ok, pair)
        dst = sums[:, bass.ds(block * width, width)]
        nc.vector.tensor_tensor(dst, bank(b), dst, ALU.add).then_inc(z_ok, 1)
    return add


def conv_out(nc, s, a):
    wt, wz, ld_ok, t_ok, t_sb, mm_ok, x_ok, dv, w_ok = (s.sem(n) for n in
        ("weights", "weights_zero", "res_loaded", "t_ok", "t_sb", "mm_ok", "x_ok", "dve_step", "w_ok"))
    loaded = [s.sem("res_loaded") for _ in range(2)]
    res = s.work[:, 0:512].rearrange("p (u f) -> p u f", u=2)
    zT = s.work[:, 512:1536].rearrange("p (u q n) -> p u q n", u=2, q=4)
    aout = s.work[:, 1536:1536 + BLOCKS]
    zb = s.work[:, 2048:3072].rearrange("p (u f) -> p u f", u=2)
    zc = s.sem("z_copied")
    w = s.wk[:, 0:1024].rearrange("p (q f) -> p q f", q=4)
    parts = [("lin2_w00", 0), ("lin2_w11", 1), ("lin2_w11", 2), ("lin2_w11", 3),
             ("lin2_w10", 1), ("lin2_w10", 2), ("lin2_w10", 3), ("lin2_w01", 0)]
    with nc.Block() as block:
        @block.sync
        def _(sp):
            sp.wait_ge(wz, 1)
            for n, (name, o) in enumerate(parts):
                sp.dma_start(w[n % 2 * 64:n % 2 * 64 + 64, n // 2, o * MUL:(o + 1) * MUL], a[name]).then_inc(wt, 16)

            def tile(k, u):
                if not peeled(k, 2):
                    sp.wait_ge(x_ok, k - 1)
                sp.dma_start(res[:, u, :], s.res_rows[bass.ds(k * P, P), :]).then_inc(loaded[u], 16)
            run_tiles(sp, BLOCKS, 2, tile)

        @block.tensor
        def _(pe):
            pe.wait_ge(w_ok, 1)

            def tile(k, u):
                pe.wait_ge(zc, k + 1)
                if not peeled(k, 2):
                    pe.wait_ge(t_sb, k - 1)
                for q in range(4):
                    last = nc.tensor.transpose(s.ps[:, u, q * P:(q + 1) * P], zb[:, u, q * P:(q + 1) * P], s.ident[:, :])
                last.then_inc(t_ok, 1)
                pe.wait_ge(t_sb, k + 1)
                if not peeled(k, 2):
                    pe.wait_ge(x_ok, k - 1)
                for q in range(4):
                    last = nc.tensor.matmul(s.ps[:, 2 + u, 0:FEAT], zT[:, u, q, :], w[:, q, :], start=(q == 0), stop=(q == 3))
                last.then_inc(mm_ok, 1)
            run_tiles(pe, BLOCKS, 2, tile)

        @block.scalar
        def _(act):
            def tile(k, u):
                if not peeled(k, 2):
                    act.wait_ge(t_ok, k - 1)
                nc.scalar.activation(zb[:, u, :], s.z[:, bass.ds(k * 512, 512)], ACT.Copy).then_inc(zc, 1)
            run_tiles(act, BLOCKS, 2, tile)

        @block.vector
        def _(dve):
            v = nc.vector
            step = Chain(dve, dv)
            v.memset(s.wk[:, 0:1024], 0.0).then_inc(wz, 1)
            step(v.tensor_scalar(aout, s.acol[:, :], AGG_SCALE, None, ALU.mult))
            dve.wait_ge(wt, 16 * 8)
            v.tensor_scalar(w[64:128, 3, 0:MUL], w[64:128, 3, 0:MUL], 1.0 / math.sqrt(3.0), None, ALU.mult).then_inc(w_ok, 1)

            def tile(k, u):
                dve.wait_ge(t_ok, k + 1)
                if not peeled(k, 2):
                    dve.wait_ge(mm_ok, k - 1)
                v.tensor_copy(zT[:, u, :, :].rearrange("p q n -> p (q n)"), s.ps[:, u, :]).then_inc(t_sb, 1)
                dve.wait_ge(mm_ok, k + 1)
                dve.wait_ge(loaded[u], (k - u) * 8 + 16)
                sc = aout[:, bass.ds(k, 1)]
                row = s.xr[:, bass.ds(k, 1), :].rearrange("p o f -> p (o f)")
                ps = s.ps[:, 2 + u, 0:FEAT]
                dve.wait_ge(zc, k + 1)
                v.scalar_tensor_tensor(row[:, 0:MUL], ps[:, 0:MUL], sc, res[:, u, 0:MUL], ALU.mult, ALU.add)
                v.scalar_tensor_tensor(row[:, MUL:].rearrange("p (u c) -> p c u", c=3), ps[:, MUL:].rearrange("p (c u) -> p c u", c=3), sc,
                                       res[:, u, MUL:].rearrange("p (u c) -> p c u", c=3), ALU.mult, ALU.add).then_inc(x_ok, 1)
            run_tiles(dve, BLOCKS, 2, tile)


def per_head(col, width):
    return col.unsqueeze(2).broadcast_to([P, HEADS, width])


def aggregate(nc, s, dve, k, row, hrow, tmp, rec, steps):
    v = nc.vector
    sums = s.sums[:, bass.ds(k * ROW, ROW)]
    own = s.exself[:, bass.ds(k, 1), :].rearrange("p o h -> p (o h)")
    r3 = lambda t: t.rearrange("p (h f) -> p h f", h=HEADS)
    steps(v.tensor_tensor(r3(tmp), r3(hrow), per_head(own, HID + 1), ALU.mult))
    steps(v.tensor_tensor(tmp, tmp, sums, ALU.add))
    steps(v.reciprocal(rec, r3(tmp)[:, :, HID]))
    steps(v.tensor_tensor(r3(row), r3(tmp)[:, :, 0:HID], per_head(rec, HID), ALU.mult))
    steps(v.tensor_tensor(row, row, s.bias[:, 0, :], ALU.add))


def gat_nodes(nc, s, a, layer):
    names = "wt prep_t prep_sb prep_mm prep_ok in_ok t_ok t_sb mm_ok mm_used dve_step one_ok neg_ok exp_ok bias_ok att_z att_ok"
    q = {n: s.sem(n) for n in names.split()}
    stored = [s.sem("h_stored") for _ in range(2)]
    loaded = [s.sem("h_loaded") for _ in range(2)]
    as_stored = s.sem("as_stored")
    wk = s.work
    hc = wk[:, 0:512].rearrange("p (u f) -> p u f", u=2)
    hT = wk[:, 512:1024].rearrange("p (u h n) -> p u h n", u=2, h=2)
    hrow = wk[:, 1024:1544].rearrange("p (u f) -> p u f", u=2)
    own = wk[:, 1544:2064].rearrange("p (u f) -> p u f", u=2)
    tmp, rec = wk[:, 2064:2324], wk[:, 2324:2328]
    neg = wk[:, 2328:2840].rearrange("p (u f) -> p u f", u=2)
    wT = wk[:, 3072:3584].rearrange("p (i o) -> p i o", i=2)
    w = s.wk[:, 0:528].rearrange("p (h f) -> p h f", h=2)
    att = s.wk[:, 528:544].rearrange("p (h f) -> p h f", h=2)
    name = str(layer)

    def widths(u):
        return [(s.ps[:, 2 + u, 0:264], [(h, w[:, h, :]) for h in range(2)])]

    pe_tile, copy_t = project(nc, s, lambda u: hc[:, u, :], q["in_ok"], None, widths, q["t_ok"], q["t_sb"], q["mm_ok"], q["mm_used"], hT)
    with nc.Block() as block:
        @block.sync
        def _(sp):
            sp.dma_start(w[:, :, 0:FEAT], a["W" + name].rearrange("(h p) f -> p h f", p=P)).then_inc(q["wt"], 16)
            sp.wait_ge(q["att_z"], 1)
            with nc.allow_non_contiguous_dma(reason="512 words, once"):
                for n, kind in enumerate(("src", "dst")):
                    for h in range(HEADS):
                        sp.dma_start(att[h % 2 * 64:h % 2 * 64 + 64, h // 2, n * 4 + h:n * 4 + h + 1],
                                     a[f"att_{kind}{name}"][h:h + 1, :].rearrange("o c -> c o")).then_inc(q["wt"], 16)
            if layer == 2:
                sp.dma_start(s.bias[:, 0, :], a["b1"].rearrange("(o n) -> o n", o=1).broadcast_to([P, FEAT])).then_inc(q["bias_ok"], 16)

            def load(k, u):
                sp.dma_start(own[:, u, :], s.h_rows[bass.ds(k * P, P), :]).then_inc(loaded[u], 16)

            def tile(k, u):
                if layer == 2:
                    if not peeled(k, 2):
                        sp.wait_ge(q["in_ok"], k - 1)
                    load(k, u)
                if peeled(k, 2) and k == 0:
                    return
                store(k - 1, 1 - u)

            def store(k, u):
                sp.wait_ge(q["one_ok"], k + 1)
                sp.wait_ge(q["mm_used"], k + 1)
                sp.dma_start(s.h_rows[bass.ds(k * P, P), :], hrow[:, u, :]).then_inc(stored[u], 16)
                sp.dma_start(s.as_rows[bass.ds(k * P, P), :], s.asd[:, bass.ds(k, 1), 0:HEADS].rearrange("p o h -> p (o h)")).then_inc(as_stored, 16)
            run_tiles(sp, BLOCKS, 2, tile)
            store(BLOCKS - 1, (BLOCKS - 1) % 2)
            for u in range(2):
                sp.wait_ge(stored[u], 16 * ((BLOCKS + 1 - u) // 2))
            sp.wait_ge(as_stored, 16 * BLOCKS)

        @block.scalar
        def _(act):
            def tile(k, u):
                if layer == 1:
                    if not peeled(k, 2):
                        act.wait_ge(q["t_ok"], k - 1)
                    normed(nc, s, hc[:, u, :], k, False).then_inc(q["in_ok"], 1)
                else:
                    act.wait_ge(q["neg_ok"], k + 1)
                    nc.scalar.activation(neg[:, u, :], neg[:, u, :], ACT.Exp).then_inc(q["exp_ok"], 1)
            run_tiles(act, BLOCKS, 2, tile)

        @block.tensor
        def _(pe):
            pe.wait_ge(q["wt"], 16 * 9)
            for i in range(2):
                for o in range(2):
                    last = nc.tensor.transpose(s.ps[:, 4, (o * 2 + i) * P:(o * 2 + i + 1) * P], w[:, i, o * P:(o + 1) * P], s.ident[:, :])
            last.then_inc(q["prep_t"], 1)
            pe.wait_ge(q["prep_sb"], 1)
            for i in range(2):
                for o in range(2):
                    last = nc.tensor.matmul(s.ps[:, 5, i * 8:i * 8 + 8], wT[:, o, i * P:(i + 1) * P], att[:, o, :], start=(o == 0), stop=(o == 1))
            last.then_inc(q["prep_mm"], 1)
            pe.wait_ge(q["prep_ok"], 1)
            run_tiles(pe, BLOCKS, 2, pe_tile(pe))

        @block.vector
        def _(dve):
            v = nc.vector
            step = Chain(dve, q["dve_step"])
            v.memset(s.wk[:, 528:544], 0.0).then_inc(q["att_z"], 1)
            step(v.memset(hrow, 1.0))
            dve.wait_ge(q["prep_t"], 1)
            v.tensor_copy(wT.rearrange("p i o -> p (i o)"), s.ps[:, 4, :]).then_inc(q["prep_sb"], 1)
            dve.wait_ge(q["prep_mm"], 1)
            v.tensor_copy(w[:, :, FEAT:FEAT + 8], s.ps[:, 5, 0:16].rearrange("p (h f) -> p h f", h=2)).then_inc(q["prep_ok"], 1)
            if layer == 2:
                dve.wait_ge(q["bias_ok"], 16)
            count, per = s.sem("agg_step"), 6

            def tile(k, u):
                if layer == 2:
                    dve.wait_ge(loaded[u], (k - u) * 8 + 16)
                    if not peeled(k, 2):
                        dve.wait_ge(q["t_ok"], k - 1)
                    n = [0]

                    def steps(ins, last=False):
                        n[0] += 1
                        ins.then_inc(count, 1)
                        dve.wait_ge(count, k * per + n[0])
                    row = hc[:, u, :]
                    aggregate(nc, s, dve, k, row, own[:, u, :], tmp, rec, steps)
                    v.tensor_scalar(neg[:, u, :], row, 0.0, None, ALU.min).then_inc(q["neg_ok"], 1)
                    steps(v.tensor_scalar(row, row, 0.0, None, ALU.max))
                    dve.wait_ge(q["exp_ok"], k + 1)
                    v.scalar_tensor_tensor(row, neg[:, u, :], -1.0, row, ALU.add, ALU.add).then_inc(q["in_ok"], 1)
                copy_t(dve, k, u)
                dve.wait_ge(q["mm_ok"], k + 1)
                if not peeled(k, 2):
                    dve.wait_ge(stored[u], (k - u) * 8)
                ps = s.ps[:, 2 + u, :]
                v.tensor_copy(hrow[:, u, :].rearrange("p (h f) -> p h f", h=HEADS)[:, :, 0:HID],
                              ps[:, 0:FEAT].rearrange("p (h f) -> p h f", h=HEADS)).then_inc(q["one_ok"], 1)
                v.tensor_copy(s.asd[:, bass.ds(k, 1), :].rearrange("p o h -> p (o h)"), ps[:, FEAT:FEAT + 8]).then_inc(q["mm_used"], 1)
            run_tiles(dve, BLOCKS, 2, tile)


def gat_scores(nc, s):
    idx_ok, batch_ok, dv, pl, z_ok = (s.sem(n) for n in ("idx_ok", "batch_ok", "dve_step", "pool_step", "zeroed"))
    BATCH = 32
    batches = GATHERED // BATCH
    groups = (-(-TILES // BATCH) * BATCH - GATHERED) // LOOKED_UP
    assert batches % 2 == 0 and groups > 3
    got = s.swdge("got_scores", 2, [batches // 2 * BATCH * 16] * 2)
    base = s.sums
    by_edge = base[:, 0:ROWS * 4].rearrange("p (t h) -> p t h", h=4)
    fwd = base[:, 0:ROWS * 4].rearrange("p (h e) -> p h e", h=4)
    inter = base[:, ROWS * 4:ROWS * 8].rearrange("p (e h) -> p e h", h=4)
    first8 = base[:, 0:ROWS * 8].rearrange("p (e q) -> p e q", q=8)
    score = base[:, ROWS * 8:ROWS * 12].rearrange("p (h e) -> p h e", h=4)
    fill = base[:, ROWS * 12:ROWS * 14].rearrange("p (n e) -> p n e", n=2)
    o = ROWS * 4
    hi_t = base[:, o:o + ROWS]
    picked = base[:, o + ROWS:o + ROWS + 2 * LOOKED_UP * 4 * BLOCKS].rearrange("p (u n) -> p u n", u=2)
    hi_i = picked[:, 0, 0:ROWS].bitcast(I32)
    o += ROWS + 2 * LOOKED_UP * 4 * BLOCKS
    mask = base[:, o:o + 2 * LOOKED_UP * BLOCKS].rearrange("p (u t n) -> p u t n", u=2, n=BLOCKS)
    o += 2 * LOOKED_UP * BLOCKS
    parts = base[:, o:o + 6 * BLOCKS].bitcast(BF16).rearrange("p (q n) -> p q n", q=3)
    p_f = base[:, o + 6 * BLOCKS:o + 6 * BLOCKS + 1]
    rest, wide_part = picked[:, 1, 0:4 * BLOCKS], picked[:, 1, 4 * BLOCKS:8 * BLOCKS]
    lo_bc = s.work[:, 2048:4096].bitcast(BF16).rearrange("p (u e) -> p u e", u=2)
    hot = s.ring[:, :, :].rearrange("p r f -> p (r f)")[:, 0:2048].bitcast(BF16).rearrange("p (u e) -> p u e", u=2)
    hot_ok, table_ok, row_in, mask_ok, pick_ok, sum_ok = (s.sem(n) for n in
        ("hot_ok", "table_ok", "row_in", "mask_ok", "pick_ok", "sum_ok"))
    lo_in = [s.sem("lo_in") for _ in range(2)]
    by_slot = base[:, 0:SLOT_CHUNKS * 512].rearrange("p (c e) -> p c e", e=512)
    stage = s.work[:, 0:2 * BATCH].bitcast(I32).rearrange("p (u n) -> p u n", u=2)
    ringa = s.work[:, 64:64 + 2 * BATCH * 4].rearrange("p (u n) -> p u n", u=2)
    amax = s.work[:, 512:512 + BLOCKS * 4].rearrange("p (k h) -> p k h", h=4)
    t4 = s.work[:, 768:768 + BLOCKS * 4].rearrange("p (k h) -> p k h", h=4)
    lasts = s.work[:, 1024:1024 + CHUNKS * 8].rearrange("p (c q) -> p c q", q=8)
    carry = s.work[:, 1088:1088 + CHUNKS * 8].rearrange("p (c q) -> p c q", q=8)
    line = s.work[0:8, 1152:1152 + ROWS + 1]
    line_in = s.work[0:8, 2560:2560 + ROWS]
    tr_ok, row_ok, last_ok, lineT, line_ok, carry_t, carry_ok = (s.sem(n) for n in
        ("tr_ok", "row_ok", "last_ok", "line_t", "line_ok", "carry_t", "carry_ok"))
    max_made, max_st, node_ok, self_ok, got_first = (s.sem(n) for n in
        ("max_made", "max_stored", "node_ok", "self_ok", "got_first"))
    z4_ok, e_ok, ex_st, ext, exs = (s.sem(n) for n in ("z4_ok", "e_ok", "ex_stored", "ex_t", "ex_s"))
    (got_max, max0), = s.swdge("got_max", 1, [16 * BLOCKS])
    (sc_st, sc0), = s.swdge("scattered", 1, [16 * BLOCKS])
    (got_ex, ex0), = s.swdge("got_ex", 1, [16 * SLOT_CHUNKS])
    ps = s.ps

    with nc.Block() as block:
        @block.gpsimd
        def _(pool):
            def batch(g, u):
                pool_wait(pool, s, idx_ok, g + 1)
                if not peeled(g, 2):
                    pool_wait(pool, s, batch_ok, g - 1)
                for n in range(BATCH):
                    pool.indirect_dma_start(out=ringa[:, u, 4 * n:4 * n + 4], out_offset=None, in_=s.as_rows,
                                            in_offset=bass.IndirectOffsetOnAxis(ap=stage[:, u, n:n + 1], axis=0)).then_inc(got[u][0], 16)
            run_tiles(pool, batches, 2, batch)
            pool.wait_ge(max_st, 16 * CHUNKS)
            for k in range(BLOCKS):
                pool.indirect_dma_start(out=amax[:, k, :], out_offset=None, in_=s.max_rows,
                                        in_offset=bass.IndirectOffsetOnAxis(ap=s.last_i[:, k:k + 1], axis=0)).then_inc(got_max, 16)
            pool.wait_ge(node_ok, 1)
            for k in range(BLOCKS):
                pool.indirect_dma_start(out=s.fill_rows, out_offset=bass.IndirectOffsetOnAxis(ap=s.first_i[:, k:k + 1], axis=0),
                                        in_=s.node8[:, k, :], in_offset=None,
                                        bounds_check=ROWS * P - 1, oob_is_err=False).then_inc(sc_st, 16)
            pool.wait_ge(ex_st, 16 * CHUNKS)
            for c in range(SLOT_CHUNKS):
                pool.indirect_dma_start(out=by_slot[:, c, :], out_offset=None, in_=s.ex_rows,
                                        in_offset=bass.IndirectOffsetOnAxis(ap=s.t_slot[:, c:c + 1], axis=0)).then_inc(got_ex, 16)

        @block.sync
        def _(sp):
            lines = s.lo_rows.rearrange("(t k) e -> t (k e)", k=LOOKED_UP)

            def load(j, u):
                if not peeled(j, 2):
                    sp.wait_ge(hot_ok, j - 1)
                sp.dma_start(lo_bc[:, u, :], lines[bass.ds(GATHERED // LOOKED_UP + j, 1), :].broadcast_to([P, LOOKED_UP * P])).then_inc(lo_in[u], 16)
            run_tiles(sp, groups, 2, load)
            sp.wait_ge(max_made, 1)
            rows = s.max_rows.rearrange("(c p e) h -> c p (e h)", p=P, e=P)
            for c in range(CHUNKS):
                sp.dma_start(rows[c], inter[:, c * P:(c + 1) * P, :].rearrange("p e h -> p (e h)")).then_inc(max_st, 16)
            sp.wait_ge(sc_st, 16 * BLOCKS + sc0)
            rows = s.fill_rows.rearrange("(c p e) q -> c p (e q)", p=P, e=P)
            for c in range(CHUNKS):
                sp.dma_start(first8[:, c * P:(c + 1) * P, :].rearrange("p e q -> p (e q)"), rows[c]).then_inc(got_first, 16)
            sp.wait_ge(e_ok, 1)
            rows = s.ex_rows.rearrange("(c p) (h e) -> c p h e", p=P, e=P)
            for c in range(CHUNKS):
                sp.dma_start(rows[c], score[:, :, c * P:(c + 1) * P]).then_inc(ex_st, 16)
            sp.wait_ge(ex_st, 16 * CHUNKS)

        @block.scalar
        def _(act):
            def put(g, u):
                if not peeled(g, 2):
                    act.wait_ge(batch_ok, g - 1)
                nc.scalar.activation(stage[:, u, :], s.src_t[:, bass.ds(g * BATCH, BATCH)], ACT.Copy).then_inc(idx_ok, 1)

            def take(g, u):
                act.wait_ge(got[u][0], ((g - u) * 8 + 16) * BATCH + got[u][1])
                nc.scalar.activation(by_edge[:, bass.ds(g * BATCH, BATCH), :].rearrange("p t h -> p (t h)"), ringa[:, u, :], ACT.Copy).then_inc(batch_ok, 1)
            for u in range(2):
                put(u, u)
            take(0, 0)

            put(2, 0)
            take(1, 1)
            put(3, 1)
            with act.Fori(1, batches // 2 - 1) as i:
                for u in range(2):
                    take(i * 2 + u, u)
                    put(i * 2 + u + 2, u)
            for g in range(batches // 2 * 2 - 2, batches):
                take(g, g % 2)
            act.wait_ge(z_ok, 1)
            for c in range(CHUNKS):
                act.wait_ge(tr_ok, c + 1)
                nc.scalar.activation(score[:, :, c * P:(c + 1) * P], ps[:, c % 2, :].rearrange("p (h e) -> p h e", h=4), ACT.Copy).then_inc(row_ok, 1)
            act.wait_ge(node_ok, 2)
            nc.scalar.activation(s.exself[:, :, :], s.exself[:, :, :], ACT.Exp).then_inc(self_ok, 1)
            act.wait_ge(z4_ok, 1)
            nc.scalar.activation(score, score, ACT.Exp).then_inc(e_ok, 1)
            for c in range(SLOT_CHUNKS):
                act.wait_ge(ext, c + 1)
                nc.scalar.activation(s.edge_x[:, :, c * P:(c + 1) * P], ps[:, 6 + c % 2, :].rearrange("p (h e) -> p h e", h=4), ACT.Copy).then_inc(exs, 1)

        @block.tensor
        def _(pe):
            t = nc.tensor
            pe.wait_ge(table_ok, 1)

            def look_up(j, u):
                pe.wait_ge(hot_ok, j + 1)
                for i in range(LOOKED_UP // 2):
                    n = j * (LOOKED_UP // 2) + i
                    if not (isinstance(j, int) and n < 8):
                        pe.wait_ge(pick_ok, n - 7)
                    for k in range(2):
                        e = (2 * i + k) * P
                        for q in range(3):
                            last = t.matmul(ps[:, i, k * 4 * BLOCKS:(k + 1) * 4 * BLOCKS], hot[:, u, e:e + P], parts[:, q, :],
                                            start=(k == 0 and q == 0), stop=(k == 1 and q == 2), skip_group_check=True)
                    last.then_inc(row_in, 1)
            run_tiles(pe, groups, 2, look_up)
            pe.wait_ge(sum_ok, groups)
            pe.wait_ge(batch_ok, batches)
            pe.wait_ge(z_ok, 1)
            for c in range(CHUNKS):
                if c >= 2:
                    pe.wait_ge(row_ok, c - 1)
                for h in range(HEADS):
                    last = t.transpose(ps[:, c % 2, h * P:(h + 1) * P], by_edge[:, c * P:(c + 1) * P, h], s.ident[:, :])
                last.then_inc(tr_ok, 1)
            for n, w in ((1, 4), (2, 8)):
                pe.wait_ge(last_ok, n)
                for c in range(CHUNKS):
                    last = t.transpose(ps[0:w, 2 + c // 4, c % 4 * P:c % 4 * P + P], lasts[:, c, 0:w], s.ident[:, :])
                last.then_inc(lineT, 1)
                pe.wait_ge(line_ok, n)
                for c in range(CHUNKS):
                    last = t.transpose(ps[:, 4, c * 8:c * 8 + w], line[0:w, c * P:(c + 1) * P], s.ident[0:w, 0:w])
                last.then_inc(carry_t, 1)
            for c in range(SLOT_CHUNKS):
                pe.wait_ge(got_ex, 16 * SLOT_CHUNKS + ex0)
                if c >= 2:
                    pe.wait_ge(exs, c - 1)
                for h in range(HEADS):
                    last = t.transpose(ps[:, 6 + c % 2, h * P:(h + 1) * P], by_slot[:, c, h * P:(h + 1) * P], s.ident[:, :])
                last.then_inc(ext, 1)

        @block.vector
        def _(dve):
            v = nc.vector
            step = Chain(dve, dv)
            v.memset(by_edge[:, GATHERED + groups * LOOKED_UP:ROWS, :], 0.0).then_inc(z_ok, 1)
            step(v.tensor_copy(rest.rearrange("p (h k) -> p h k", h=4), s.asd[:, :, 0:4].rearrange("p k h -> p h k")))
            for q in range(3):
                step(v.tensor_copy(parts[:, q, :], rest))
                if q < 2:
                    step(v.tensor_copy(wide_part, parts[:, q, :]))
                    step(v.tensor_tensor(rest, rest, wide_part, ALU.subtract))
            step(v.tensor_scalar(hi_i, s.src_t[:, :], 7, None, ALU.logical_shift_right))
            step(v.tensor_copy(hi_t, hi_i))
            step(v.tensor_tensor(wide_part[:, 0:P], s.ident[:, :], s.iota[:, :], ALU.mult))
            v.tensor_reduce(p_f, wide_part[:, 0:P], AX.X, ALU.add).then_inc(table_ok, 1)
            dve.wait_ge(table_ok, 1)

            def one_hot(j, u):
                dve.wait_ge(lo_in[u], (j - u) * 8 + 16)
                if not peeled(j, 2):
                    dve.wait_ge(row_in, (j - 1) * (LOOKED_UP // 2))
                v.tensor_scalar(hot[:, u, :], lo_bc[:, u, :], p_f, None, ALU.is_equal).then_inc(hot_ok, 1)

            def add_up(j, u):
                dve.wait_ge(pick_ok, (j + 1) * (LOOKED_UP // 2))
                v.tensor_reduce(by_edge[:, bass.ds(GATHERED + j * LOOKED_UP, LOOKED_UP), :].rearrange("p t h -> p (t h)"),
                                picked[:, u, :].rearrange("p (t k) -> p t k", k=BLOCKS), AX.X, ALU.add).then_inc(sum_ok, 1)

            def pick(j, u, final=False):
                hi = hi_t[:, bass.ds(GATHERED + j * LOOKED_UP, LOOKED_UP)]
                v.tensor_tensor(mask[:, u, :, :], s.iota[:, 0:BLOCKS].unsqueeze(1).broadcast_to([P, LOOKED_UP, BLOCKS]),
                                hi.unsqueeze(2).broadcast_to([P, LOOKED_UP, BLOCKS]), ALU.is_equal).then_inc(mask_ok, 1)
                if not final:
                    one_hot(j + 1, 1 - u)
                if not (isinstance(j, int) and j == 0):
                    add_up(j - 1, 1 - u)
                dve.wait_ge(mask_ok, j + 1)
                if not peeled(j, 2):
                    dve.wait_ge(sum_ok, j - 1)
                for i in range(LOOKED_UP // 2):
                    dve.wait_ge(row_in, j * (LOOKED_UP // 2) + i + 1)
                    m = mask[:, u, 2 * i:2 * i + 2, :].unsqueeze(2).broadcast_to([P, 2, 4, BLOCKS])
                    v.tensor_tensor(picked[:, u, i * 8 * BLOCKS:(i + 1) * 8 * BLOCKS].rearrange("p (t h k) -> p t h k", t=2, h=4),
                                    ps[:, i, 0:8 * BLOCKS].rearrange("p (t h k) -> p t h k", t=2, h=4), m, ALU.mult).then_inc(pick_ok, 1)
            one_hot(0, 0)
            run_tiles(dve, groups - 1, 2, pick)
            pick(groups - 1, (groups - 1) % 2, True)
            add_up(groups - 1, (groups - 1) % 2)
            dve.wait_ge(row_ok, CHUNKS)
            for h in range(HEADS):
                last = v.tensor_tensor_scan(fwd[:, h, :], s.dmax[:, :], score[:, h, :], -BIG, ALU.add, ALU.max)
            step(last)

            def carries(n, w, keep, initial, op0, op1):
                dve.wait_ge(lineT, n)
                step(v.tensor_copy(line_in[0:w, 0:512], ps[0:w, 2, :]))
                step(v.tensor_copy(line_in[0:w, 512:ROWS], ps[0:w, 3, 0:ROWS - 512]))
                step(v.memset(line[0:w, 0:1], initial))
                v.tensor_tensor_scan(line[0:w, 1:ROWS + 1], keep[0:w, :], line_in[0:w, :], initial, op0, op1).then_inc(line_ok, 1)
                dve.wait_ge(carry_t, n)
                step(v.tensor_copy(carry[:, :, 0:w], ps[:, 4, 0:CHUNKS * 8].rearrange("p (c q) -> p c q", q=8)[:, :, 0:w]))

            v.tensor_copy(lasts[:, :, 0:4], fwd.rearrange("p h (c e) -> p c h e", e=P)[:, :, :, P - 1]).then_inc(last_ok, 1)
            carries(1, 4, s.dmax_r, -BIG, ALU.add, ALU.max)
            for c in range(CHUNKS):
                for h in range(HEADS):
                    part = slice(c * P, (c + 1) * P)
                    last = v.scalar_tensor_tensor(inter[:, part, h], s.npre[:, part], carry[:, c, h:h + 1], fwd[:, h, part], ALU.add, ALU.max)
            last.then_inc(max_made, 1)
            dve.wait_ge(got_max, 16 * BLOCKS + max0)
            a_s, a_d = s.asd[:, :, 0:4], s.asd[:, :, 4:8]
            wide = lambda t: t[:, :].unsqueeze(2).broadcast_to([P, BLOCKS, 4])
            step(v.tensor_tensor(amax, amax, wide(s.has), ALU.mult))
            step(v.tensor_tensor(amax, amax, wide(s.hasb), ALU.add))
            step(v.tensor_tensor(amax, amax, a_s, ALU.max))
            step(v.tensor_tensor(amax, amax, a_d, ALU.add))
            step(v.tensor_copy(s.node8[:, :, 0:4], a_d))
            v.scalar_tensor_tensor(s.node8[:, :, 4:8], amax, 0.2, amax, ALU.mult, ALU.max).then_inc(node_ok, 1)
            dve.wait_ge(node_ok, 1)
            step(v.tensor_tensor(t4, a_s, a_d, ALU.add))
            step(v.scalar_tensor_tensor(amax, t4, 0.2, t4, ALU.mult, ALU.max))
            v.tensor_tensor(s.exself[:, :, :], amax, s.node8[:, :, 4:8], ALU.subtract).then_inc(node_ok, 1)
            dve.wait_ge(got_first, 16 * CHUNKS)
            for n in range(8):
                step(v.tensor_tensor_scan(fill[:, 0, :], s.keep[:, :], first8[:, :, n], 0.0, ALU.mult, ALU.add))
                last = v.tensor_copy(lasts[:, :, n], fill[:, 0, :].rearrange("p (c e) -> p c e", e=P)[:, :, P - 1])
                if n < 7:
                    step(last)
            last.then_inc(last_ok, 1)
            dve.wait_ge(last_ok, 2)
            carries(2, 8, s.keep_r, 0.0, ALU.mult, ALU.add)
            for h in range(HEADS):
                for m in range(2):
                    step(v.tensor_tensor_scan(fill[:, m, :], s.keep[:, :], first8[:, :, h + 4 * m], 0.0, ALU.mult, ALU.add))
                    for c in range(CHUNKS):
                        part = slice(c * P, (c + 1) * P)
                        last = v.scalar_tensor_tensor(fill[:, m, part], s.pre[:, part], carry[:, c, h + 4 * m:h + 4 * m + 1],
                                                      fill[:, m, part], ALU.mult, ALU.add)
                    step(last)
                step(v.tensor_tensor(score[:, h, :], score[:, h, :], fill[:, 0, :], ALU.add))
                step(v.scalar_tensor_tensor(fill[:, 0, :], score[:, h, :], 0.2, score[:, h, :], ALU.mult, ALU.max))
                step(v.tensor_tensor(fill[:, 0, :], fill[:, 0, :], fill[:, 1, :], ALU.subtract))
                last = v.tensor_scalar(score[:, h, :], fill[:, 0, :], 0.0, None, ALU.min)
                if h < HEADS - 1:
                    step(last)
            last.then_inc(z4_ok, 1)


def gat_edges(nc, s):
    idx_ok, msg_ok, sel_ok, agg_ok, zero_ok, z_ok = (s.sem(n) for n in
        ("idx_ok", "msg_ok", "sel_ok", "agg_ok", "zero_ok", "z_ok"))
    got = s.swdge("ring", RING, [SLOTS // RING * 16] * RING)
    msg = s.work[:, 0:4 * ROW].rearrange("p (b k f) -> p b k f", b=2, k=2)
    sel = s.work[:, 2048:2048 + 4 * P].rearrange("p (b k n) -> p b k n", b=2, k=2)
    with nc.Block() as block:
        @block.gpsimd
        def _(pool):
            gather_slots(pool, s, s.h_rows, ROW, idx_ok, got, msg_ok)

        @block.scalar
        def _(act):
            def stage(g, u):
                if not peeled(g, 2):
                    act.wait_ge(msg_ok, (g - 1) * 8)
                nc.scalar.activation(s.idx[:, u, :], s.src_x[:, bass.ds(g * GROUP, GROUP)], ACT.Copy).then_inc(idx_ok, 1)
            run_tiles(act, GROUPS, 2, stage)

        @block.tensor
        def _(pe):
            def collect(g, q):
                pair, b = g * 8 + q, q % 2
                pe.wait_ge(msg_ok, pair + 1)
                pe.wait_ge(sel_ok, pair + 1)
                if not (isinstance(g, int) and g == 0 and q < 2):
                    pe.wait_ge(z_ok, pair - 1)
                for k in range(2):
                    last = nc.tensor.matmul(s.ps[:, b, 0:ROW], sel[:, b, k, :], msg[:, b, k, :], start=(k == 0), stop=(k == 1))
                last.then_inc(agg_ok, 1)

            def group(g, u):
                for q in range(8):
                    collect(g, q)
            run_tiles(pe, GROUPS, 2, group)

        @block.vector
        def _(dve):
            v = nc.vector
            v.memset(s.sums, 0.0).then_inc(zero_ok, 1)
            dve.wait_ge(zero_ok, 1)

            def make(g, q):
                pair, b = g * 8 + q, q % 2
                if not (isinstance(g, int) and g == 0 and q < 2):
                    dve.wait_ge(agg_ok, pair - 1)
                for k in range(2):
                    last = v.tensor_scalar(sel[:, b, k, :], s.iota[:, :], s.dst_x[:, bass.ds(pair * 2 + k, 1)], None, ALU.is_equal)
                last.then_inc(sel_ok, 1)
                landed(dve, got, g, 2 * q)
                landed(dve, got, g, 2 * q + 1)
                r = 2 * q % RING
                ex = s.edge_x[:, :, bass.ds(pair * 2, 2)].rearrange("p h k -> p k h").unsqueeze(3).broadcast_to([P, 2, HEADS, HID + 1])
                v.tensor_tensor(msg[:, b, :, :].rearrange("p k (h f) -> p k h f", h=HEADS),
                                s.ring[:, r:r + 2, :].rearrange("p k (h f) -> p k h f", h=HEADS), ex, ALU.mult).then_inc(msg_ok, 1)

            add8 = adder(nc, s, dve, s.sums, agg_ok, z_ok, ROW, lambda b: s.ps[:, b, 0:ROW])

            def group(g, u):
                for q in range(8):
                    make(g, q)
                    if isinstance(g, int) and g == 0 and q == 0:
                        continue
                    if q:
                        add8(g, (q - 1) // 2, (q - 1) % 2)
                    else:
                        add8(g - 1, 3, 1)
            run_tiles(dve, GROUPS, 2, group)
            add8(GROUPS - 1, 3, 1)


def gat_out(nc, s, a, out):
    bias_ok, neg_ok, exp_ok, count, out_ok = (s.sem(n) for n in ("bias_ok", "neg_ok", "exp_ok", "agg_step", "out_ok"))
    loaded = [s.sem("h_loaded") for _ in range(2)]
    stored = [s.sem("stored") for _ in range(2)]
    wk = s.work
    own = wk[:, 0:520].rearrange("p (u f) -> p u f", u=2)
    row = wk[:, 520:1032].rearrange("p (u f) -> p u f", u=2)
    neg = wk[:, 1032:1544].rearrange("p (u f) -> p u f", u=2)
    tmp, rec = wk[:, 1544:1804], wk[:, 1804:1808]
    with nc.Block() as block:
        @block.sync
        def _(sp):
            sp.dma_start(s.bias[:, 0, :], a["b2"].rearrange("(o n) -> o n", o=1).broadcast_to([P, FEAT])).then_inc(bias_ok, 16)

            def load(k, u):
                if not peeled(k, 2):
                    sp.wait_ge(out_ok, k - 1)
                sp.dma_start(own[:, u, :], s.h_rows[bass.ds(k * P, P), :]).then_inc(loaded[u], 16)
            run_tiles(sp, BLOCKS, 2, load)

        @block.scalar
        def _(act):
            def tile(k, u):
                act.wait_ge(neg_ok, k + 1)
                nc.scalar.activation(neg[:, u, :], neg[:, u, :], ACT.Exp).then_inc(exp_ok, 1)
                act.wait_ge(out_ok, k + 1)
                n = min(P, NODES - k * P) if isinstance(k, int) else P
                act.dma_start(out[bass.ds(k * P, n), :], row[0:n, u, :]).then_inc(stored[u], 16)
            run_tiles(act, BLOCKS, 2, tile)
            for u in range(2):
                act.wait_ge(stored[u], 16 * ((BLOCKS + 1 - u) // 2))

        @block.vector
        def _(dve):
            v = nc.vector
            dve.wait_ge(bias_ok, 16)
            per = 7

            def tile(k, u):
                dve.wait_ge(loaded[u], (k - u) * 8 + 16)
                if not peeled(k, 2):
                    dve.wait_ge(stored[u], (k - u) * 8)
                n = [0]

                def steps(ins):
                    n[0] += 1
                    ins.then_inc(count, 1)
                    dve.wait_ge(count, k * per + n[0])
                r = row[:, u, :]
                aggregate(nc, s, dve, k, r, own[:, u, :], tmp, rec, steps)
                v.tensor_scalar(neg[:, u, :], r, 0.0, None, ALU.min).then_inc(neg_ok, 1)
                steps(v.scalar_tensor_tensor(r, r, 0.0, s.xr[:, bass.ds(k, 1), :].rearrange("p o f -> p (o f)"), ALU.max, ALU.add))
                dve.wait_ge(exp_ok, k + 1)
                steps(v.tensor_scalar(neg[:, u, :], neg[:, u, :], -1.0, None, ALU.add))
                v.tensor_tensor(r, r, neg[:, u, :], ALU.add).then_inc(out_ok, 1)
            run_tiles(dve, BLOCKS, 2, tile)


def kernel(**inputs):
    import numpy as np
    import concourse.bacc as bacc
    from concourse.bass_utils import run_bass_kernel_spmd

    def get(name):
        return np.ascontiguousarray(inputs[name])

    def rows(x, count, fill):
        x = np.asarray(x)
        full = np.full((count,) + x.shape[1:], fill, x.dtype)
        full[:x.shape[0]] = x
        return full

    none = BLOCKS * P
    dst = rows(get("dst"), ROWS * P, none)
    src = rows(get("src"), ROWS * P, 0)
    prev = np.concatenate([np.full(1, -1, dst.dtype), dst[:-1]])
    ea4 = rows(get("edge_attr_4"), ROWS * P, 0).reshape(ROWS, P, 4)
    ea8 = rows(get("edge_attr_8"), ROWS * P, 0).reshape(ROWS, P, 8)
    arrays = {
        "x": rows(get("x"), BLOCKS * P, 0),
        "a_cols": rows(get("node_vec1"), BLOCKS * P, 0).reshape(BLOCKS, P).T,
        "dst_rows": dst.reshape(ROWS, P),
        "prev_rows": prev.reshape(ROWS, P),
        "src_t": src.reshape(ROWS, P).T,
        "sd_rows": np.concatenate([src.reshape(ROWS, P), dst.reshape(ROWS, P)], 1),
        "ea4_rows": ea4.transpose(0, 2, 1).reshape(ROWS, 4 * P),
        "ea8_rows": ea8.transpose(0, 2, 1).reshape(ROWS * 8, P),
    }
    for n in ("sc_w0", "sc_w1", "lin1_w0", "lin1_w1", "fc_w1", "fc_w2", "lin2_w00", "lin2_w01", "lin2_w10", "lin2_w11"):
        arrays[n] = get("L0_gnn_" + n)
    for n in ("W1", "att_src1", "att_dst1", "b1", "W2", "att_src2", "att_dst2", "b2"):
        arrays[n] = get("L1_gnn_" + n)
    arrays = {n: np.ascontiguousarray(v) for n, v in arrays.items()}
    nc = bacc.Bacc("TRN2", target_bir_lowering=False, num_devices=1)
    a = {n: nc.dram_tensor("in_" + n, v.shape, mybir.dt.from_np(v.dtype), kind="ExternalInput").ap() for n, v in arrays.items()}
    out = nc.dram_tensor("out", (NODES, FEAT), F32, kind="ExternalOutput").ap()
    build(nc, a, out)
    result = run_bass_kernel_spmd(nc, [{"in_" + n: v for n, v in arrays.items()}], core_ids=[0])
    return result.results[0]["out"]
```

```python
import math
from contextlib import ExitStack

import concourse.bass as bass
from concourse import mybir

F32 = mybir.dt.float32
I32 = mybir.dt.int32
BF16 = mybir.dt.bfloat16
ALU = mybir.AluOpType
ACT = mybir.ActivationFunctionType
AX = mybir.AxisListType

P = 128
NODES, EDGES, FEAT = 6250, 106250, 256
MUL, HEADS, HID = 64, 4, 64
BLOCKS = -(-NODES // P)
TILES = -(-EDGES // P)
PAIRS = -(-TILES // 2)
STEPS = PAIRS + BLOCKS - 1
SLOTS = 2 * STEPS
CHUNKS = -(-TILES // P)
ROWS = CHUNKS * P
SLOT_CHUNKS = -(-SLOTS // P)
SLOT_COLS = SLOT_CHUNKS * P
GROUP = 16
GROUPS = SLOTS // GROUP
ROW = HEADS * (HID + 1)
GATHERED = 256
LOOKED_UP = 16
RING = 8
BIG = 1e30
assert BLOCKS % 7 == 0 and SLOTS % (2 * GROUP) == 0 and TILES < ROWS

IN_SCALE = 1.0 / math.sqrt(MUL)
AGG_SCALE = (1.679 / math.sqrt(64)) / math.sqrt(20.0) / math.sqrt(2 * MUL) * math.cos(math.pi / 8.0)
SELF_SCALE = math.sin(math.pi / 8.0)


def run_tiles(eng, n, unroll, body):
    for k in range(min(unroll, n)):
        body(k, k)
    if n // unroll > 1:
        with eng.Fori(1, n // unroll) as i:
            for u in range(unroll):
                body(i * unroll + u, u)
    for k in range(max(unroll, n // unroll * unroll), n):
        body(k, k % unroll)


def run_ahead(eng, n, ahead, body, unroll=2):
    def both(k, u):
        ahead(k + 1, (u + 1) % unroll)
        body(k, u)
    ahead(0, 0)
    run_tiles(eng, n - 1, unroll, both)
    body(n - 1, (n - 1) % unroll)


def peeled(k, unroll):
    return isinstance(k, int) and k < unroll


class Chain:

    def __init__(self, eng, sem):
        self.eng, self.sem, self.n = eng, sem, 0

    def __call__(self, ins):
        self.n += 1
        ins.then_inc(self.sem, 1)
        self.eng.wait_ge(self.sem, self.n)


def build(nc, a, out):
    ctx = ExitStack()
    with ctx:
        names = {}

        def sb(name, shape, dt=F32):
            return ctx.enter_context(nc.sbuf_tensor(name, shape, dt))

        def sem(name):
            names[name] = names.get(name, 0) + 1
            held = s.phase.enter_context(nc.semaphore(f"{name}_{names[name]}"))
            s.phase_sems.append(held)
            return held

        def dram(name, shape, dt=F32):
            return nc.dram_tensor(name, shape, dt, kind="Internal").ap()

        class S:
            pass

        s = S()
        s.sent = {}

        def swdge(name, n, counts):
            if name not in s.sent:
                s.sent[name] = [[ctx.enter_context(nc.semaphore(f"{name}{i}")), 0] for i in range(n)]
            before = [(x[0], x[1]) for x in s.sent[name]]
            for x, c in zip(s.sent[name], counts):
                x[1] += c
            return before
        s.swdge = swdge
        s.passed = ctx.enter_context(nc.semaphore("waits_passed"))
        s.sb, s.sem, s.dram = sb, sem, dram
        s.y_rows = dram("y_rows", (BLOCKS * P, FEAT))
        s.res_rows = dram("res_rows", (BLOCKS * P, FEAT))
        s.h_rows = dram("h_rows", (BLOCKS * P, ROW))
        s.as_rows = dram("as_rows", (BLOCKS * P, HEADS))
        s.max_rows = dram("max_rows", (ROWS * P, HEADS))
        s.fill_rows = dram("fill_rows", (ROWS * P, 2 * HEADS))
        s.ex_rows = dram("ex_rows", (ROWS, HEADS * P))
        s.lo_rows = dram("lo_rows", (ROWS, P), BF16)
        s.first_line = dram("first_line", (BLOCKS * P + 1, 1))
        s.block_line = dram("block_line", (SLOT_COLS, 1), I32)
        s.ident = sb("ident", [P, P])
        s.ones = sb("ones", [P, P])
        s.iota = sb("iota", [P, P])
        s.acol = sb("acol", [P, BLOCKS])
        s.src_t = sb("src_t", [P, ROWS], I32)
        s.src_x = sb("src_x", [P, SLOT_COLS], I32)
        s.dst_x = sb("dst_x", [P, SLOT_COLS])
        s.edge_x = sb("edge_x", [P, 4, SLOT_COLS])
        s.blk = sb("blk", [1, SLOT_COLS], I32)
        s.idx8 = sb("idx8", [P, GROUPS], I32)
        s.t_slot = sb("t_slot", [P, SLOT_CHUNKS], I32)
        s.keep = sb("keep", [P, ROWS])
        s.dmax = sb("dmax", [P, ROWS])
        s.pre = sb("pre", [P, ROWS])
        s.npre = sb("npre", [P, ROWS])
        s.n0 = sb("n0", [P, CHUNKS])
        s.keep_r = sb("keep_r", [8, ROWS])
        s.dmax_r = sb("dmax_r", [8, ROWS])
        s.first_i = sb("first_i", [P, BLOCKS], I32)
        s.last_i = sb("last_i", [P, BLOCKS], I32)
        s.has = sb("has", [P, BLOCKS])
        s.hasb = sb("hasb", [P, BLOCKS])
        s.stat = sb("stat", [P, BLOCKS, 2])
        s.rstd = sb("rstd", [P, BLOCKS])
        s.nmr = sb("nmr", [P, BLOCKS])
        s.asd = sb("asd", [P, BLOCKS, 8])
        s.exself = sb("exself", [P, BLOCKS, HEADS])
        s.z = sb("z", [P, BLOCKS * (FEAT + ROW)])
        s.xr = s.z[:, 0:BLOCKS * FEAT].rearrange("p (k f) -> p k f", f=FEAT)
        s.sums = s.z[:, BLOCKS * FEAT:BLOCKS * (FEAT + ROW)]
        s.work = sb("work", [P, 4096])
        s.ring = sb("ring", [P, RING, ROW])
        s.idx = sb("idx", [P, 2, GROUP], I32)
        s.wk = sb("wk", [P, 2048])
        s.w8 = sb("w8", [P, 8 * P])
        s.w2 = sb("w2", [P, 2 * FEAT])
        s.bias = sb("bias", [P, 2, FEAT])
        s.ps = ctx.enter_context(nc.psum_tensor("ps", [P, 8, 512], F32))
        phase(nc, s, setup, a)
        phase(nc, s, norm_stats, a["x"])
        phase(nc, s, conv_nodes, a)
        phase(nc, s, conv_edges, a)
        phase(nc, s, conv_out, a)
        phase(nc, s, norm_stats)
        for layer in (1, 2):
            phase(nc, s, gat_nodes, a, layer)
            phase(nc, s, gat_scores)
            phase(nc, s, gat_edges)
        phase(nc, s, gat_out, a, out)


def phase(nc, s, program, *args):
    with ExitStack() as s.phase:
        s.phase_sems = []
        program(nc, s, *args)
        with nc.Block() as block:
            @block.gpsimd
            def _(pool):
                for used in s.phase_sems:
                    pool.sem_clear(used)


def setup(nc, s, a):
    loaded, zeroed, made, put, st_blk, got_blk = (s.sem(n) for n in ("loaded", "zeroed", "made", "put", "st_blk", "got_blk"))
    iotas, pl, dv, pe, ac = (s.sem(n) for n in ("iotas", "pool_step", "dve_step", "pe_step", "act_step"))
    st_first, got_next = s.sem("st_first"), s.sem("got_next")
    (g_rows, _), = s.swdge("got_rows", 1, [0])
    (g_sd, _), = s.swdge("got_ints", 1, [0])
    (g_e4, _), = s.swdge("got_floats", 1, [0])
    mm_q, q_ok, mm_last, slot_idx, qi_ok = (s.sem(n) for n in ("mm_q", "q_ok", "mm_last", "slot_idx", "qi_ok"))
    rs_t, rs_sb, re_t, src_ok, tr, ev = (s.sem(n) for n in ("rs_t", "rs_sb", "re_t", "src_ok", "tr", "ev"))
    hs_ok, hs_t, blk_ok, oddb_ok, lb_ok = (s.sem(n) for n in ("hs_ok", "hs_t", "blk_ok", "oddb_ok", "lb_ok"))
    pe_tr = s.sem("pe_tr")
    z = s.z
    o = [0]

    def part(n, dt=F32, shape=None):
        v = z[:, o[0]:o[0] + n]
        o[0] += n
        if dt is not F32:
            v = v.bitcast(dt)
        return v.rearrange(shape[0], **shape[1]) if shape else v

    rows = ("p (c e) -> p c e", dict(e=P))
    d_r = part(ROWS, I32)
    d_p = part(ROWS, I32)
    d1 = part(ROWS)
    cmp = part(58 * 48)
    last_b = part(ROWS)
    last_all = part(ROWS)
    dg = part(BLOCKS * P, I32)
    sd = part(SLOT_CHUNKS * 256, I32, ("p (c e) -> p c e", dict(e=256)))
    e4 = part(SLOT_CHUNKS * 512, F32, ("p (c e) -> p c e", dict(e=512)))
    srcf = part(SLOT_COLS)
    dstf = part(SLOT_COLS)
    zt = part(ROWS * 2)
    sm = part(1300)
    assert o[0] <= BLOCKS * (FEAT + ROW)
    m = [0]

    def small(n, dt=F32):
        v = sm[:, m[0]:m[0] + n]
        m[0] += n
        return v if dt is F32 else v.bitcast(dt)

    io_f, io_p, j_i, jg_i, n_i = small(P, I32), small(1, I32), small(SLOT_CHUNKS, I32), small(GROUPS, I32), small(BLOCKS, I32)
    pi, pf = small(8, I32), small(8)
    lastd, thr, cnt, qb, io48 = small(CHUNKS), small(48), small(48), small(48), small(48)
    jf, bf, tf, negb = (small(SLOT_CHUNKS) for _ in range(4))
    jg, bg, tg = (small(GROUPS) for _ in range(3))
    nf, q, cn, rs, re = (small(BLOCKS) for _ in range(5))
    qi, hs, bi = small(BLOCKS, I32), small(CHUNKS), small(SLOT_CHUNKS, I32)
    hsb = small(CHUNKS * 8)
    tr49 = small(P)
    oddb = s.wk[:, 0:P]
    etile = small(1)
    nxt = small(P)
    lo_ok, src_in = s.sem("lo_ok"), s.sem("src_in")
    src_r, lo_i = s.work[:, 0:ROWS].bitcast(I32), s.work[:, ROWS:2 * ROWS].bitcast(I32)
    lo_b = s.work[:, 2 * ROWS:2 * ROWS + ROWS // 2].bitcast(BF16)

    with nc.Block() as block:
        @block.sync
        def _(sp):
            for dst, src in ((d_r, a["dst_rows"]), (d_p, a["prev_rows"])):
                sp.dma_start(dst.rearrange("p (c e) -> p c e", e=P),
                             src.rearrange("(c p) e -> p c e", p=P)).then_inc(loaded, 16)
            sp.dma_start(s.src_t[:, :], a["src_t"]).then_inc(made, 16)
            sp.dma_start(src_r.rearrange("p (c e) -> p c e", e=P),
                         a["sd_rows"][:, 0:P].rearrange("(c p) e -> p c e", p=P)).then_inc(src_in, 16)
            sp.dma_start(s.acol[:, :], a["a_cols"]).then_inc(made, 16)
            sp.wait_ge(zeroed, 1)
            fill = s.fill_rows.rearrange("(h p r) q -> h p (r q)", p=P, h=4)
            for h in range(4):
                sp.dma_start(fill[h], zt).then_inc(put, 16)
            sp.wait_ge(lo_ok, 1)
            sp.dma_start(s.lo_rows.rearrange("(c p) e -> p c e", p=P), lo_b.rearrange("p (c e) -> p c e", e=P)).then_inc(put, 16)
            sp.wait_ge(blk_ok, 1)
            with nc.allow_non_contiguous_dma(reason="1024 words, once"):
                sp.dma_start(s.block_line.rearrange("(c p) o -> p (c o)", p=P), bi).then_inc(st_blk, 16)
            sp.wait_ge(st_blk, 16)
            sp.dma_start(s.blk[:, :], s.block_line.rearrange("n o -> o n")).then_inc(got_blk, 16)
            sp.wait_ge(rs_sb, 1)
            sp.dma_start(s.first_line[0:BLOCKS * P, :].rearrange("(k p) o -> k (p o)", p=P), tr49[0:BLOCKS, :]).then_inc(st_first, 16)
            sp.dma_start(s.first_line[BLOCKS * P:BLOCKS * P + 1, :], etile[0:1, :]).then_inc(st_first, 16)
            sp.wait_ge(st_first, 32)
            sp.dma_start(nxt[0:BLOCKS, :], s.first_line[1:BLOCKS * P + 1, :].rearrange("(k p) o -> k (p o)", p=P)).then_inc(got_next, 16)
            sp.wait_ge(got_next, 16)
            sp.wait_ge(got_blk, 16)
            sp.wait_ge(made, 32)
            sp.wait_ge(put, 80)

        @block.gpsimd
        def _(pool):
            step = Chain(pool, pl)
            pool.iota(io_f, [[1, P]], base=0, channel_multiplier=0).then_inc(iotas, 1)
            pool.iota(io_p, [[1, 1]], base=0, channel_multiplier=1).then_inc(iotas, 1)
            pool.iota(j_i, [[64, SLOT_CHUNKS]], base=0, channel_multiplier=0).then_inc(iotas, 1)
            pool.iota(jg_i, [[8, GROUPS]], base=0, channel_multiplier=0).then_inc(iotas, 1)
            pool.iota(n_i, [[P, BLOCKS]], base=0, channel_multiplier=1).then_inc(iotas, 1)
            pool.memset(s.ones[:, :], 1.0).then_inc(iotas, 1)
            step(pool.memset(s.ident[:, :], 0.0))
            pool.affine_select(out=s.ident[:, :], in_=s.ident[:, :], compare_op=ALU.not_equal, fill=1.0,
                               base=0, pattern=[[-1, P]], channel_multiplier=1).then_inc(iotas, 1)
            pool.wait_ge(slot_idx, 1)
            for c in range(SLOT_CHUNKS):
                for dst, src, got in ((sd, a["sd_rows"], g_sd), (e4, a["ea4_rows"], g_e4)):
                    pool.indirect_dma_start(out=dst[:, c, :], out_offset=None, in_=src,
                                            in_offset=bass.IndirectOffsetOnAxis(ap=s.t_slot[:, c:c + 1], axis=0)).then_inc(got, 16)
            for k in range(BLOCKS):
                pool.wait_ge(qi_ok, k // 7 + 1)
                pool.indirect_dma_start(out=dg[:, k * P:(k + 1) * P], out_offset=None, in_=a["dst_rows"],
                                        in_offset=bass.IndirectOffsetOnAxis(ap=qi[:, k:k + 1], axis=0)).then_inc(g_rows, 16)

        @block.vector
        def _(dve):
            step = Chain(dve, dv)
            v = nc.vector
            v.memset(zt, 0.0).then_inc(zeroed, 1)
            step(v.memset(etile[0:1, :], float(EDGES)))
            dve.wait_ge(iotas, 7)
            step(v.tensor_copy(s.iota[:, :], io_f))
            for n, (op, by, op2, by2) in enumerate(((ALU.logical_shift_right, 1, None, None), (ALU.bitwise_and, 1, None, None),
                                                    (ALU.logical_shift_right, 4, None, None), (ALU.logical_shift_right, 3, ALU.bitwise_and, 1),
                                                    (ALU.bitwise_and, 7, None, None))):
                if op2 is None:
                    step(v.tensor_scalar(pi[:, n:n + 1], io_p, by, None, op))
                else:
                    step(v.tensor_scalar(pi[:, n:n + 1], io_p, by, by2, op, op2))
            step(v.tensor_copy(pf[:, 0:5], pi[:, 0:5]))
            half, odd, p16, p8odd, p_and7 = (pf[:, n:n + 1] for n in range(5))
            v.tensor_copy(oddb, odd.broadcast_to([P, P])).then_inc(oddb_ok, 1)
            step(v.tensor_copy(nf, n_i))
            dve.wait_ge(src_in, 16)
            step(v.tensor_scalar(lo_i, src_r, P - 1, None, ALU.bitwise_and))
            v.tensor_copy(lo_b, lo_i).then_inc(lo_ok, 1)
            dve.wait_ge(loaded, 32)
            keep3, d13 = (t.rearrange("p (c e) -> p c e", e=P) for t in (s.keep[:, :], d1))
            step(v.tensor_tensor(s.keep[:, :], d_r, d_p, ALU.not_equal))
            step(v.tensor_reduce(hs, keep3, AX.X, ALU.max))
            v.tensor_copy(hsb.rearrange("p (c h) -> p c h", h=8), hs.unsqueeze(2).broadcast_to([P, CHUNKS, 8])).then_inc(hs_ok, 1)
            step(v.tensor_scalar(s.keep[:, :], s.keep[:, :], -1.0, 1.0, ALU.mult, ALU.add))
            step(v.memset(d1, 0.0))
            step(v.tensor_copy(d13[:, :, 0:1], keep3[:, :, 0:1]))
            step(v.tensor_scalar(s.n0[:, :], keep3[:, :, 0], -1.0, BIG, ALU.add, ALU.mult))
            step(v.memset(keep3[:, :, 0:1], 0.0))
            step(v.tensor_scalar(s.dmax[:, :], s.keep[:, :], -1.0, BIG, ALU.add, ALU.mult))
            step(v.tensor_tensor_scan(s.pre[:, :], s.keep[:, :], d1, 0.0, ALU.mult, ALU.max))
            step(v.tensor_scalar(s.npre[:, :], s.pre[:, :], -1.0, BIG, ALU.add, ALU.mult))
            step(v.tensor_copy(lastd, d_r.rearrange("p (c e) -> p c e", e=P)[:, :, P - 1]))
            v.tensor_copy(last_b.rearrange("p (c e) -> p c e", e=P), lastd.unsqueeze(2).broadcast_to([P, CHUNKS, P])).then_inc(lb_ok, 1)
            step(v.tensor_scalar(thr, s.iota[:, 0:48], 1.0, float(P), ALU.add, ALU.mult))
            c3 = cmp[:, 0:48 * CHUNKS].rearrange("p (b c) -> p b c", c=CHUNKS)
            step(v.tensor_tensor(c3, lastd.unsqueeze(1).broadcast_to([P, 48, CHUNKS]), thr.unsqueeze(2).broadcast_to([P, 48, CHUNKS]), ALU.is_lt))
            v.tensor_reduce(cnt, c3, AX.X, ALU.add).then_inc(q_ok, 1)
            step(v.tensor_scalar(jf, j_i, half, None, ALU.add))
            step(v.tensor_scalar(jg, jg_i, p16, None, ALU.add))
            dve.wait_ge(mm_q, 1)
            step(v.tensor_scalar(qb, s.ps[:, 0, 0:48], float(PAIRS - 1), None, ALU.min))
            step(v.tensor_tensor(qb, qb, s.iota[:, 0:48], ALU.add))
            for n, jv, bv in ((SLOT_CHUNKS, jf, bf), (GROUPS, jg, bg)):
                c3 = cmp[:, 0:n * 48].rearrange("p (j b) -> p j b", b=48)
                step(v.tensor_tensor(c3, qb.unsqueeze(1).broadcast_to([P, n, 48]), jv.unsqueeze(2).broadcast_to([P, n, 48]), ALU.is_lt))
                step(v.tensor_reduce(bv, c3, AX.X, ALU.add))
            v.tensor_copy(bi, bf).then_inc(blk_ok, 1)
            step(v.tensor_scalar(negb, bf, -float(P), None, ALU.mult))
            step(v.tensor_tensor(tf, jf, bf, ALU.subtract))
            step(v.tensor_scalar(tf, tf, 2.0, odd, ALU.mult, ALU.add))
            v.tensor_scalar(s.t_slot[:, :], tf, float(ROWS - 1), None, ALU.min).then_inc(slot_idx, 1)
            step(v.tensor_tensor(tg, jg, bg, ALU.subtract))
            step(v.tensor_scalar(tg, tg, 2.0, p8odd, ALU.mult, ALU.add))
            step(v.tensor_scalar(s.idx8[:, :], tg, 8.0, p_and7, ALU.mult, ALU.add))
            dve.wait_ge(mm_last, 1)
            step(v.tensor_copy(last_all[:, 0:512], s.ps[:, 1, 0:512]))
            step(v.tensor_copy(last_all[:, 512:ROWS], s.ps[:, 2, 0:ROWS - 512]))
            for k in range(BLOCKS):
                step(v.tensor_scalar(d1, last_all, nf[:, k:k + 1], None, ALU.is_lt, ALU.add, accum_out=q[:, k:k + 1]))
                if k % 7 == 6:
                    v.tensor_scalar(qi[:, k - 6:k + 1], q[:, k - 6:k + 1], float(ROWS - 1), None, ALU.min).then_inc(qi_ok, 1)
            dve.wait_ge(g_sd, 16 * SLOT_CHUNKS)
            step(v.tensor_copy(srcf.rearrange("p (c e) -> p c e", e=P), sd[:, :, 0:P]))
            for c in range(SLOT_CHUNKS):
                v.tensor_scalar(dstf[:, c * P:(c + 1) * P], sd[:, c, P:2 * P], negb[:, c:c + 1], None, ALU.add).then_inc(tr, 1)
            dve.wait_ge(g_rows, 16 * BLOCKS)
            dg3 = dg.rearrange("p (k e) -> p k e", e=P)
            dgf = dg.bitcast(F32).rearrange("p (k e) -> p k e", e=P)
            step(v.tensor_tensor(dgf, dg3, nf.unsqueeze(2).broadcast_to([P, BLOCKS, P]), ALU.is_lt))
            step(v.tensor_reduce(cn, dgf, AX.X, ALU.add))
            v.scalar_tensor_tensor(rs, q, float(P), cn, ALU.mult, ALU.add).then_inc(src_ok, 1)
            dve.wait_ge(rs_t, 1)
            v.tensor_copy(tr49[0:BLOCKS, :], s.ps[0:BLOCKS, 0, 0:P]).then_inc(rs_sb, 1)
            dve.wait_ge(re_t, 1)
            step(v.tensor_copy(re, s.ps[:, 4, 0:BLOCKS]))
            step(v.tensor_tensor(s.has[:, :], re, rs, ALU.is_gt))
            step(v.tensor_scalar(s.hasb[:, :], s.has[:, :], -1.0, BIG, ALU.add, ALU.mult))
            step(v.tensor_scalar(s.last_i[:, :], re, -1.0, 0.0, ALU.add, ALU.max))
            step(v.tensor_scalar(cn, s.has[:, :], -1.0, -float(1 << 20), ALU.add, ALU.mult))
            step(v.tensor_tensor(s.first_i[:, :], rs, cn, ALU.add))
            dve.wait_ge(hs_t, 1)
            for b, lo, n in ((5, 0, 512), (6, 512, ROWS - 512)):
                step(v.tensor_scalar(s.keep_r[:, lo:lo + n], s.ps[0:8, b, 0:n], -1.0, 1.0, ALU.mult, ALU.add))
            step(v.tensor_scalar(s.dmax_r[:, :], s.keep_r[:, :], -1.0, BIG, ALU.add, ALU.mult))

        @block.tensor
        def _(pe):
            t = nc.tensor
            pe.wait_ge(oddb_ok, 1)
            pe.wait_ge(q_ok, 1)
            t.matmul(s.ps[:, 0, 0:48], oddb, cnt, start=True, stop=True).then_inc(mm_q, 1)
            pe.wait_ge(lb_ok, 1)
            for c in range(CHUNKS):
                last = t.matmul(s.ps[:, 1 + c // 4, c % 4 * P:c % 4 * P + P], last_b[:, c * P:(c + 1) * P], s.ident[:, :], start=True, stop=True)
            last.then_inc(mm_last, 1)
            pe.wait_ge(hs_ok, 1)
            for c in range(CHUNKS):
                last = t.transpose(s.ps[0:8, 5 + c // 4, c % 4 * P:c % 4 * P + P], hsb[:, c * 8:c * 8 + 8], s.ident[:, :])
            last.then_inc(hs_t, 1)
            pe.wait_ge(mm_q, 1)
            pe.wait_ge(tr, SLOT_CHUNKS)
            pe.wait_ge(g_e4, 16 * SLOT_CHUNKS)
            pe.wait_ge(dv, 1)
            for c in range(SLOT_CHUNKS):
                if c >= 1:
                    pe.wait_ge(ev, c)
                t.transpose(s.ps[:, 7, 0:P], srcf[:, c * P:(c + 1) * P], s.ident[:, :])
                last = t.transpose(s.ps[:, 7, P:2 * P], dstf[:, c * P:(c + 1) * P], s.ident[:, :])
                last.then_inc(pe_tr, 1)
                for q4 in range(4):
                    last = t.transpose(s.ps[:, 3, q4 * P:(q4 + 1) * P], e4[:, c, q4 * P:(q4 + 1) * P], s.ident[:, :])
                last.then_inc(pe_tr, 1)
            pe.wait_ge(src_ok, 1)
            t.transpose(s.ps[0:BLOCKS, 0, 0:P], rs, s.ident[:, :]).then_inc(rs_t, 1)
            pe.wait_ge(got_next, 16)
            t.transpose(s.ps[:, 4, 0:BLOCKS], nxt[0:BLOCKS, :], s.ident[0:BLOCKS, 0:BLOCKS]).then_inc(re_t, 1)

        @block.scalar
        def _(act):
            for c in range(SLOT_CHUNKS):
                act.wait_ge(pe_tr, 2 * c + 2)
                nc.scalar.activation(s.src_x[:, c * P:(c + 1) * P], s.ps[:, 7, 0:P], ACT.Copy)
                nc.scalar.activation(s.dst_x[:, c * P:(c + 1) * P], s.ps[:, 7, P:2 * P], ACT.Copy)
                nc.scalar.activation(s.edge_x[:, :, c * P:(c + 1) * P],
                                     s.ps[:, 3, :].rearrange("p (q e) -> p q e", e=P), ACT.Copy).then_inc(ev, 1)


def norm_stats(nc, s, x=None):
    dv, var_ok, sd_ok, x_ok = (s.sem(n) for n in ("dve_step", "var_ok", "sd_ok", "x_ok"))
    var = s.stat[:, :, 1]
    six = s.wk[:, 0:BLOCKS * 6].rearrange("p (k q) -> p k q", q=6)
    with nc.Block() as block:
        if x is not None:
            @block.sync
            def _(sp):
                sp.dma_start(s.xr, x.rearrange("(k p) f -> p k f", p=P)).then_inc(x_ok, 16)

        @block.vector
        def _(dve):
            step = Chain(dve, dv)
            if x is not None:
                dve.wait_ge(x_ok, 16)
            for k in range(BLOCKS):
                last = nc.vector.bn_stats(six[:, k, :], s.xr[:, k, :])
            step(last)
            for k in range(BLOCKS):
                last = nc.vector.bn_aggr(s.stat[:, k, :], six[:, k, :])
            step(last)
            nc.vector.tensor_scalar(s.rstd[:, :], var, 1e-5, None, ALU.add).then_inc(var_ok, 1)
            dve.wait_ge(sd_ok, 1)
            step(nc.vector.reciprocal(s.rstd[:, :], s.nmr[:, :]))
            nc.vector.scalar_tensor_tensor(s.nmr[:, :], s.stat[:, :, 0], -1.0, s.rstd[:, :], ALU.mult, ALU.mult)

        @block.scalar
        def _(act):
            act.wait_ge(var_ok, 1)
            nc.scalar.activation(s.nmr[:, :], s.rstd[:, :], ACT.Sqrt).then_inc(sd_ok, 1)


def normed(nc, s, dst, k, split):
    kw = dict(bias=s.nmr[:, bass.ds(k, 1)], scale=s.rstd[:, bass.ds(k, 1)])
    row = s.xr[:, bass.ds(k, 1), :].rearrange("p o f -> p (o f)")
    if not split:
        return nc.scalar.activation(dst, row, ACT.Relu, **kw)
    nc.scalar.activation(dst[:, 0:MUL], row[:, 0:MUL], ACT.Relu, **kw)
    return nc.scalar.activation(dst[:, MUL:].rearrange("p (c u) -> p u c", c=3),
                                row[:, MUL:].rearrange("p (u c) -> p u c", c=3), ACT.Relu, **kw)


def project(nc, s, src_of, src_ready, src_used, widths, t_ok, t_sb, mm_ok, mm_used, hT):
    def pe_tile(pe):
        def transpose(k, u):
            pe.wait_ge(src_ready, k + 1)
            if not peeled(k, 2):
                pe.wait_ge(t_sb, k - 1)
            for h in range(2):
                last = nc.tensor.transpose(s.ps[:, u, h * P:(h + 1) * P], src_of(u)[:, h * P:(h + 1) * P], s.ident[:, :])
            last.then_inc(t_ok, 1)

        def multiply(k, u):
            pe.wait_ge(t_sb, k + 1)
            if not peeled(k, 2):
                pe.wait_ge(mm_used, k - 1)
            for out, parts in widths(u):
                for n, (half, w) in enumerate(parts):
                    last = nc.tensor.matmul(out, hT[:, u, half, :], w, start=(n == 0), stop=(n == len(parts) - 1))
            last.then_inc(mm_ok, 1)
        return transpose, multiply

    def copy_t(dve, k, u):
        dve.wait_ge(t_ok, k + 1)
        if not peeled(k, 2):
            dve.wait_ge(mm_ok, k - 1)
        nc.vector.tensor_copy(hT[:, u, :, :].rearrange("p h n -> p (h n)"), s.ps[:, u, 0:FEAT]).then_inc(t_sb, 1)
    return pe_tile, copy_t


def conv_nodes(nc, s, a):
    wt, wz, hc_ok, t_ok, t_sb, mm_ok, mm_used, y_ok = (s.sem(n) for n in
        ("weights", "weights_zero", "hc_ok", "t_ok", "t_sb", "mm_ok", "mm_used", "y_ok"))
    stored = [s.sem("y_stored") for _ in range(2)]
    dv, sc_ok = s.sem("dve_step"), s.sem("scales")
    wk = s.work
    hc = wk[:, 0:512].rearrange("p (u f) -> p u f", u=2)
    hT = wk[:, 512:1024].rearrange("p (u h n) -> p u h n", u=2, h=2)
    ysb = wk[:, 1024:1536].rearrange("p (u f) -> p u f", u=2)
    ain, aself = wk[:, 1536:1536 + BLOCKS], wk[:, 1600:1600 + BLOCKS]
    res_stored = s.sem("res_stored")
    w = s.wk[:, 0:512].rearrange("p (h f) -> p h f", h=2)
    lo, hi = slice(0, MUL), slice(MUL, P)

    def widths(u):
        return [(s.ps[:, 2 + u, h * 256:(h + 1) * 256], [(h, w[:, h, :])]) for h in range(2)]

    pe_tile, copy_t = project(nc, s, lambda u: hc[:, u, :], hc_ok, None, widths, t_ok, t_sb, mm_ok, mm_used, hT)
    with nc.Block() as block:
        @block.sync
        def _(sp):
            sp.wait_ge(wz, 1)
            for h in range(2):
                for n, (rows, name) in enumerate(((lo, "lin1_w1" if h else "lin1_w0"), (hi, "lin1_w1"),
                                                  (lo, "sc_w1" if h else "sc_w0"), (hi, "sc_w1"))):
                    sp.dma_start(w[rows, h, n * MUL:(n + 1) * MUL], a[name]).then_inc(wt, 16)

            def tile(k, u):
                sp.wait_ge(y_ok, k + 1)
                sp.dma_start(s.y_rows[bass.ds(k * P, P), :], ysb[:, u, :]).then_inc(stored[u], 16)
                sp.wait_ge(mm_used, k + 1)
                sp.dma_start(s.res_rows[bass.ds(k * P, P), :], s.xr[:, bass.ds(k, 1), :].rearrange("p o f -> p (o f)")).then_inc(res_stored, 16)
            run_tiles(sp, BLOCKS, 2, tile)
            sp.wait_ge(res_stored, 16 * BLOCKS)
            for u in range(2):
                sp.wait_ge(stored[u], 16 * ((BLOCKS + 1 - u) // 2))

        @block.scalar
        def _(act):
            def tile(k, u):
                if not peeled(k, 2):
                    act.wait_ge(t_ok, k - 1)
                normed(nc, s, hc[:, u, :], k, True).then_inc(hc_ok, 1)
            run_tiles(act, BLOCKS, 2, tile)

        @block.tensor
        def _(pe):
            pe.wait_ge(wt, 16 * 8)
            run_ahead(pe, BLOCKS, *pe_tile(pe))

        @block.vector
        def _(dve):
            step = Chain(dve, dv)
            nc.vector.memset(s.wk[:, 0:512], 0.0).then_inc(wz, 1)
            step(nc.vector.tensor_scalar(ain, s.acol[:, :], IN_SCALE, None, ALU.mult))
            step(nc.vector.tensor_scalar(aself, s.acol[:, :], IN_SCALE * SELF_SCALE, None, ALU.mult))

            def tile(k, u):
                dve.wait_ge(mm_ok, k + 1)
                if not peeled(k, 2):
                    dve.wait_ge(stored[u], (k - u) * 8)
                ps = s.ps[:, 2 + u, :]
                nc.vector.tensor_scalar(ysb[:, u, :].rearrange("p (h f) -> p h f", h=2),
                                        ps.rearrange("p (h g f) -> p h g f", h=2, g=2)[:, :, 0, :],
                                        ain[:, bass.ds(k, 1)], None, ALU.mult).then_inc(y_ok, 1)
                row = s.xr[:, bass.ds(k, 1), :].rearrange("p o f -> p (o f)")
                vec = row[:, MUL:].rearrange("p (u c) -> p c u", c=3)
                sc = aself[:, bass.ds(k, 1)]
                nc.vector.scalar_tensor_tensor(row[:, 0:MUL], ps[:, 128:192], sc, row[:, 0:MUL], ALU.mult, ALU.add)
                nc.vector.scalar_tensor_tensor(vec[:, 0, :], ps[:, 192:256], sc, vec[:, 0, :], ALU.mult, ALU.add)
                nc.vector.scalar_tensor_tensor(vec[:, 1:3, :], ps[:, 384:512].rearrange("p (c u) -> p c u", c=2), sc,
                                               vec[:, 1:3, :], ALU.mult, ALU.add).then_inc(mm_used, 1)
            run_ahead(dve, BLOCKS, lambda k, u: copy_t(dve, k, u), tile)


def pool_wait(pool, s, sem, value):
    pool.wait_ge(sem, value)
    if not isinstance(value, int):
        pool.sem_inc(s.passed)


def gather_slots(pool, s, table, width, idx_ok, got, msg_ok, extra=None):
    def half(g, u):
        pool_wait(pool, s, idx_ok, g + 1)
        if extra:
            extra(g, u)
        for n in range(GROUP):
            r = n % RING
            if n % 2 == 0 and not (isinstance(g, int) and g == 0 and n < RING):
                pool_wait(pool, s, msg_ok, g * 8 + n // 2 - RING // 2 + 1)
            pool.indirect_dma_start(out=s.ring[:, r, 0:width], out_offset=None, in_=table,
                                    in_offset=bass.IndirectOffsetOnAxis(ap=s.idx[:, u, n:n + 1], axis=0)).then_inc(got[r][0], 16)
    run_tiles(pool, GROUPS, 2, half)


def landed(eng, got, g, n):
    arrived, before = got[n % RING]
    eng.wait_ge(arrived, (g * (GROUP // RING) + n // RING + 1) * 16 + before)


def conv_edges(nc, s, a):
    wt, wz, idx_ok, pre_ok, h_ok, w_ok, msg_ok, sel_ok, agg_ok, zero_ok, z_ok = (s.sem(n) for n in
        ("weights", "weights_zero", "idx_ok", "pre_ok", "h_ok", "w_ok", "msg_ok", "sel_ok", "agg_ok", "zero_ok", "z_ok"))
    eq_ok = s.sem("eq_ok")
    got = s.swdge("ring", RING, [SLOTS // RING * 16] * RING)
    got8 = s.swdge("got8_", 2, [0, 0])
    yg = s.ring[:, :, 0:FEAT]
    e8 = s.sb("e8", [P, 2, P])
    i8 = s.sb("i8", [P, 2, 1], I32)
    h2 = s.sb("h2", [P, 2, 2, P])
    msg = s.work[:, 0:2048].rearrange("p (b k f) -> p b k f", b=2, k=2)
    sel = s.work[:, 2048:4096].rearrange("p (b k c n) -> p b k c n", b=2, k=2, c=4)
    eq = s.sb("eq", [P, 2, 2, P])
    w8 = s.w8[:, :].rearrange("p (q m) -> p q m", q=8)
    ps = s.ps
    tail = (GROUPS - 1) % 2

    with nc.Block() as block:
        @block.sync
        def _(sp):
            sp.wait_ge(wz, 2)
            for n in range(GROUP):
                sp.dma_start(w8[8 * n:8 * n + 8, n // 2, n % 2 * 64:n % 2 * 64 + 64], a["fc_w1"]).then_inc(wt, 16)
            for h in range(2):
                sp.dma_start(s.w2[h * 64:(h + 1) * 64, 0:FEAT], a["fc_w2"]).then_inc(wt, 16)

        @block.gpsimd
        def _(pool):
            def scalars(g, u):
                if not peeled(g, 2):
                    pool_wait(pool, s, pre_ok, (g - 1) * 4)
                pool.indirect_dma_start(out=e8[:, u, :], out_offset=None, in_=a["ea8_rows"],
                                        in_offset=bass.IndirectOffsetOnAxis(ap=i8[:, u, :], axis=0)).then_inc(got8[u][0], 16)
            gather_slots(pool, s, s.y_rows, FEAT, idx_ok, got, msg_ok, scalars)

        @block.scalar
        def _(act):
            def stage(g, u):
                if not peeled(g, 2):
                    act.wait_ge(msg_ok, (g - 1) * 8)
                nc.scalar.activation(i8[:, u, :], s.idx8[:, bass.ds(g, 1)], ACT.Copy)
                nc.scalar.activation(s.idx[:, u, :], s.src_x[:, bass.ds(g * GROUP, GROUP)], ACT.Copy).then_inc(idx_ok, 1)

            def silu(g, q):
                n = g * 4 + q
                act.wait_ge(pre_ok, n + 1)
                if not (isinstance(g, int) and g == 0 and q < 2):
                    act.wait_ge(w_ok, 2 * (n - 1))
                nc.scalar.activation(h2[:, q % 2, :, :].rearrange("p a e -> p (a e)"), ps[:, q % 2, 0:2 * P], ACT.Silu,
                                     scale=1.0 / math.sqrt(8.0)).then_inc(h_ok, 1)

            def weights(g, q, b):
                pair = g * 8 + 2 * q + b
                act.wait_ge(eq_ok, pair + 1)
                for k in range(2):
                    slot = bass.ds(pair * 2 + k, 1)
                    for c in range(4):
                        last = nc.scalar.activation(sel[:, b, k, c, :], eq[:, b, k, :], ACT.Copy, scale=s.edge_x[:, c, slot])
                last.then_inc(sel_ok, 1)

            def group(g, u, final=False):
                for q in range(4):
                    if q < 3:
                        silu(g, q + 1)
                    elif not final:
                        silu(g + 1, 0)
                    for b in range(2):
                        weights(g, q, b)
                    if q == 1 and not final:
                        stage(g + 1, 1 - u)
            stage(0, 0)
            silu(0, 0)
            run_tiles(act, GROUPS - 1, 2, group)
            group(GROUPS - 1, tail, True)

        @block.tensor
        def _(pe):
            pe.wait_ge(wt, 16 * (GROUP + 2))

            def first(g, u, q):
                if q == 0:
                    pe.wait_ge(got8[u][0], (g - u) * 8 + 16)
                if not (isinstance(g, int) and g == 0 and q < 2):
                    pe.wait_ge(h_ok, g * 4 + q - 1)
                for b in range(2):
                    last = nc.tensor.matmul(ps[:, q % 2, b * P:(b + 1) * P], w8[:, 2 * q + b, :], e8[:, u, :], start=True, stop=True)
                last.then_inc(pre_ok, 1)

            def second(g, q, b):
                pair = g * 8 + 2 * q + b
                pe.wait_ge(h_ok, g * 4 + q + 1)
                if not (isinstance(g, int) and g == 0 and q == 0):
                    pe.wait_ge(msg_ok, pair - 1)
                for k in range(2):
                    rows = slice(64 * k, 64 * k + 64)
                    last = nc.tensor.matmul(ps[:, 2 + 2 * b + k, 0:FEAT], h2[rows, q % 2, b, :], s.w2[rows, 0:FEAT], start=True, stop=True)
                last.then_inc(w_ok, 1)

            def collect(g, q, b):
                pair = g * 8 + 2 * q + b
                pe.wait_ge(msg_ok, pair + 1)
                pe.wait_ge(sel_ok, pair + 1)
                if not (isinstance(g, int) and g == 0 and q == 0):
                    pe.wait_ge(z_ok, pair - 1)
                o = ps[:, 6 + b, :]
                for k in range(2):
                    m = msg[:, b, k, :]
                    o4, m4 = (x[:, 256:512].rearrange("p (q f) -> p q f", q=4) for x in (o, m))
                    nc.tensor.matmul(o[:, 0:256], sel[:, b, k, 0, :], m[:, 0:256], start=(k == 0), stop=False, skip_group_check=True)
                    for c in range(3):
                        last = nc.tensor.matmul(o4[:, c:4:3 - c, :], sel[:, b, k, 1 + c, :], m4[:, 0:c + 2:c + 1, :],
                                                start=False, stop=(k == 1 and c == 2), skip_group_check=True)
                last.then_inc(agg_ok, 1)

            def group(g, u, final=False):
                for q in range(4):
                    if q < 3:
                        first(g, u, q + 1)
                    elif not final:
                        first(g + 1, 1 - u, 0)
                    for b in range(2):
                        second(g, q, b)
                        if isinstance(g, int) and g == 0 and q == 0 and b == 0:
                            continue
                        if b:
                            collect(g, q, 0)
                        elif q:
                            collect(g, q - 1, 1)
                        else:
                            collect(g - 1, 3, 1)
            first(0, 0, 0)
            run_tiles(pe, GROUPS - 1, 2, group)
            group(GROUPS - 1, tail, True)
            collect(GROUPS - 1, 3, 1)

        @block.vector
        def _(dve):
            v = nc.vector
            v.memset(s.w8[:, :], 0.0).then_inc(wz, 1)
            v.memset(s.w2[:, :], 0.0).then_inc(wz, 1)
            v.memset(s.z[:, 0:BLOCKS * 512], 0.0).then_inc(zero_ok, 1)
            dve.wait_ge(zero_ok, 1)

            def select(g, q, b):
                pair = g * 8 + 2 * q + b
                if not (isinstance(g, int) and g == 0 and q == 0):
                    dve.wait_ge(agg_ok, pair - 1)
                for k in range(2):
                    last = v.tensor_scalar(eq[:, b, k, :], s.iota[:, :], s.dst_x[:, bass.ds(pair * 2 + k, 1)], None, ALU.is_equal)
                last.then_inc(eq_ok, 1)

            def messages(g, q, b):
                pair = g * 8 + 2 * q + b
                n = 4 * q + 2 * b
                dve.wait_ge(w_ok, pair + 1)
                landed(dve, got, g, n)
                landed(dve, got, g, n + 1)
                w = ps[:, 2 + 2 * b:4 + 2 * b, 0:FEAT].rearrange("p k (q f) -> p k q f", q=4)
                x = yg[:, n % RING:n % RING + 2, :]
                m = msg[:, b, :, :]
                x0 = x[:, :, 0:MUL].unsqueeze(2).broadcast_to([P, 2, 2, MUL])
                v.tensor_tensor(m.rearrange("p k (h f) -> p k h f", h=2)[:, :, :, 0:MUL], w[:, :, 0:3:2, :], x0, ALU.mult)
                x1 = x[:, :, MUL:FEAT].rearrange("p k (c f) -> p k c f", c=3)
                for lo, part in ((64, 3), (320, 1)):
                    last = v.tensor_tensor(m[:, :, lo:lo + 192].rearrange("p k (c f) -> p k c f", c=3),
                                           w[:, :, part, :].unsqueeze(2).broadcast_to([P, 2, 3, MUL]), x1, ALU.mult)
                last.then_inc(msg_ok, 1)

            add = adder(nc, s, dve, s.z, agg_ok, z_ok, 512, lambda b: ps[:, 6 + b, :])

            def group(g, u, final=False):
                for q in range(4):
                    for b in range(2):
                        messages(g, q, b)
                        if not b:
                            select(g, q, 1)
                        elif q < 3:
                            select(g, q + 1, 0)
                        elif not final:
                            select(g + 1, 0, 0)
                        if b:
                            add(g, q, 0)
                        elif q:
                            add(g, q - 1, 1)
                        elif not (isinstance(g, int) and g == 0):
                            add(g - 1, 3, 1)
            select(0, 0, 0)
            run_tiles(dve, GROUPS - 1, 2, group)
            group(GROUPS - 1, tail, True)
            add(GROUPS - 1, 3, 1)


def adder(nc, s, dve, sums, agg_ok, z_ok, width, bank):
    def add(g, q, b):
        pair = g * 8 + 2 * q + b
        block = dve.value_load(s.blk[0:1, bass.ds(pair * 2, 1)], min_val=0, max_val=BLOCKS - 1)
        dve.wait_ge(agg_ok, pair + 1)
        if not (isinstance(g, int) and g == 0 and q == 0 and b == 0):
            dve.wait_ge(z_ok, pair)
        dst = sums[:, bass.ds(block * width, width)]
        nc.vector.tensor_tensor(dst, bank(b), dst, ALU.add).then_inc(z_ok, 1)
    return add


def conv_out(nc, s, a):
    wt, wz, ld_ok, t_ok, t_sb, mm_ok, x_ok, dv, w_ok = (s.sem(n) for n in
        ("weights", "weights_zero", "res_loaded", "t_ok", "t_sb", "mm_ok", "x_ok", "dve_step", "w_ok"))
    loaded = [s.sem("res_loaded") for _ in range(2)]
    res = s.work[:, 0:512].rearrange("p (u f) -> p u f", u=2)
    zT = s.work[:, 512:1536].rearrange("p (u q n) -> p u q n", u=2, q=4)
    aout = s.work[:, 1536:1536 + BLOCKS]
    zb = s.work[:, 2048:3072].rearrange("p (u f) -> p u f", u=2)
    zc = s.sem("z_copied")
    w = s.wk[:, 0:1024].rearrange("p (q f) -> p q f", q=4)
    parts = [("lin2_w00", 0), ("lin2_w11", 1), ("lin2_w11", 2), ("lin2_w11", 3),
             ("lin2_w10", 1), ("lin2_w10", 2), ("lin2_w10", 3), ("lin2_w01", 0)]
    with nc.Block() as block:
        @block.sync
        def _(sp):
            sp.wait_ge(wz, 1)
            for n, (name, o) in enumerate(parts):
                sp.dma_start(w[n % 2 * 64:n % 2 * 64 + 64, n // 2, o * MUL:(o + 1) * MUL], a[name]).then_inc(wt, 16)

            def tile(k, u):
                if not peeled(k, 2):
                    sp.wait_ge(x_ok, k - 1)
                sp.dma_start(res[:, u, :], s.res_rows[bass.ds(k * P, P), :]).then_inc(loaded[u], 16)
            run_tiles(sp, BLOCKS, 2, tile)

        @block.tensor
        def _(pe):
            pe.wait_ge(w_ok, 1)

            def transpose(k, u):
                pe.wait_ge(zc, k + 1)
                if not peeled(k, 2):
                    pe.wait_ge(t_sb, k - 1)
                for q in range(4):
                    last = nc.tensor.transpose(s.ps[:, u, q * P:(q + 1) * P], zb[:, u, q * P:(q + 1) * P], s.ident[:, :])
                last.then_inc(t_ok, 1)

            def multiply(k, u):
                pe.wait_ge(t_sb, k + 1)
                if not peeled(k, 2):
                    pe.wait_ge(x_ok, k - 1)
                for q in range(4):
                    last = nc.tensor.matmul(s.ps[:, 2 + u, 0:FEAT], zT[:, u, q, :], w[:, q, :], start=(q == 0), stop=(q == 3))
                last.then_inc(mm_ok, 1)
            run_ahead(pe, BLOCKS, transpose, multiply)

        @block.scalar
        def _(act):
            def tile(k, u):
                if not peeled(k, 2):
                    act.wait_ge(t_ok, k - 1)
                nc.scalar.activation(zb[:, u, :], s.z[:, bass.ds(k * 512, 512)], ACT.Copy).then_inc(zc, 1)
            run_tiles(act, BLOCKS, 2, tile)

        @block.vector
        def _(dve):
            v = nc.vector
            step = Chain(dve, dv)
            v.memset(s.wk[:, 0:1024], 0.0).then_inc(wz, 1)
            step(v.tensor_scalar(aout, s.acol[:, :], AGG_SCALE, None, ALU.mult))
            dve.wait_ge(wt, 16 * 8)
            v.tensor_scalar(w[64:128, 3, 0:MUL], w[64:128, 3, 0:MUL], 1.0 / math.sqrt(3.0), None, ALU.mult).then_inc(w_ok, 1)

            def copy_t(k, u):
                dve.wait_ge(t_ok, k + 1)
                if not peeled(k, 2):
                    dve.wait_ge(mm_ok, k - 1)
                v.tensor_copy(zT[:, u, :, :].rearrange("p q n -> p (q n)"), s.ps[:, u, :]).then_inc(t_sb, 1)

            def tile(k, u):
                dve.wait_ge(mm_ok, k + 1)
                dve.wait_ge(loaded[u], (k - u) * 8 + 16)
                sc = aout[:, bass.ds(k, 1)]
                row = s.xr[:, bass.ds(k, 1), :].rearrange("p o f -> p (o f)")
                ps = s.ps[:, 2 + u, 0:FEAT]
                dve.wait_ge(zc, k + 1)
                v.scalar_tensor_tensor(row[:, 0:MUL], ps[:, 0:MUL], sc, res[:, u, 0:MUL], ALU.mult, ALU.add)
                v.scalar_tensor_tensor(row[:, MUL:].rearrange("p (u c) -> p c u", c=3), ps[:, MUL:].rearrange("p (c u) -> p c u", c=3), sc,
                                       res[:, u, MUL:].rearrange("p (u c) -> p c u", c=3), ALU.mult, ALU.add).then_inc(x_ok, 1)
            run_ahead(dve, BLOCKS, copy_t, tile)


def per_head(col, width):
    return col.unsqueeze(2).broadcast_to([P, HEADS, width])


def aggregate(nc, s, k, row, rec, steps):
    v = nc.vector
    sums = s.sums[:, bass.ds(k * ROW, ROW)].rearrange("p (h f) -> p h f", h=HEADS)
    steps(v.reciprocal(rec, sums[:, :, HID]))
    steps(v.tensor_tensor(row.rearrange("p (h f) -> p h f", h=HEADS), sums[:, :, 0:HID], per_head(rec, HID), ALU.mult))
    steps(v.tensor_tensor(row, row, s.bias[:, 0, :], ALU.add))


def gat_nodes(nc, s, a, layer):
    names = "wt prep_t prep_sb prep_mm prep_ok in_ok t_ok t_sb mm_ok mm_used dve_step one_ok neg_ok exp_ok bias_ok att_z att_ok"
    q = {n: s.sem(n) for n in names.split()}
    stored = [s.sem("h_stored") for _ in range(2)]
    as_stored = s.sem("as_stored")
    wk = s.work
    hc = wk[:, 0:512].rearrange("p (u f) -> p u f", u=2)
    hT = wk[:, 512:1024].rearrange("p (u h n) -> p u h n", u=2, h=2)
    hrow = wk[:, 1024:1544].rearrange("p (u f) -> p u f", u=2)
    rec = wk[:, 2324:2328]
    neg = wk[:, 2328:2840].rearrange("p (u f) -> p u f", u=2)
    wT = wk[:, 3072:3584].rearrange("p (i o) -> p i o", i=2)
    w = s.wk[:, 0:528].rearrange("p (h f) -> p h f", h=2)
    att = s.wk[:, 528:544].rearrange("p (h f) -> p h f", h=2)
    name = str(layer)

    def widths(u):
        return [(s.ps[:, 2 + u, 0:264], [(h, w[:, h, :]) for h in range(2)])]

    pe_tile, copy_t = project(nc, s, lambda u: hc[:, u, :], q["in_ok"], None, widths, q["t_ok"], q["t_sb"], q["mm_ok"], q["mm_used"], hT)
    with nc.Block() as block:
        @block.sync
        def _(sp):
            sp.dma_start(w[:, :, 0:FEAT], a["W" + name].rearrange("(h p) f -> p h f", p=P)).then_inc(q["wt"], 16)
            sp.wait_ge(q["att_z"], 1)
            with nc.allow_non_contiguous_dma(reason="512 words, once"):
                for n, kind in enumerate(("src", "dst")):
                    for h in range(HEADS):
                        sp.dma_start(att[h % 2 * 64:h % 2 * 64 + 64, h // 2, n * 4 + h:n * 4 + h + 1],
                                     a[f"att_{kind}{name}"][h:h + 1, :].rearrange("o c -> c o")).then_inc(q["wt"], 16)
            if layer == 2:
                sp.dma_start(s.bias[:, 0, :], a["b1"].rearrange("(o n) -> o n", o=1).broadcast_to([P, FEAT])).then_inc(q["bias_ok"], 16)

            def store(k, u):
                sp.wait_ge(q["one_ok"], k + 1)
                sp.wait_ge(q["mm_used"], k + 1)
                sp.dma_start(s.h_rows[bass.ds(k * P, P), :], hrow[:, u, :]).then_inc(stored[u], 16)
                sp.dma_start(s.as_rows[bass.ds(k * P, P), :], s.asd[:, bass.ds(k, 1), 0:HEADS].rearrange("p o h -> p (o h)")).then_inc(as_stored, 16)
            run_tiles(sp, BLOCKS, 2, store)
            for u in range(2):
                sp.wait_ge(stored[u], 16 * ((BLOCKS + 1 - u) // 2))
            sp.wait_ge(as_stored, 16 * BLOCKS)

        @block.scalar
        def _(act):
            def tile(k, u):
                if layer == 1:
                    if not peeled(k, 2):
                        act.wait_ge(q["t_ok"], k - 1)
                    normed(nc, s, hc[:, u, :], k, False).then_inc(q["in_ok"], 1)
                else:
                    act.wait_ge(q["neg_ok"], k + 1)
                    nc.scalar.activation(neg[:, u, :], neg[:, u, :], ACT.Exp).then_inc(q["exp_ok"], 1)
            run_tiles(act, BLOCKS, 2, tile)

        @block.tensor
        def _(pe):
            pe.wait_ge(q["wt"], 16 * 9)
            for i in range(2):
                for o in range(2):
                    last = nc.tensor.transpose(s.ps[:, 4, (o * 2 + i) * P:(o * 2 + i + 1) * P], w[:, i, o * P:(o + 1) * P], s.ident[:, :])
            last.then_inc(q["prep_t"], 1)
            pe.wait_ge(q["prep_sb"], 1)
            for i in range(2):
                for o in range(2):
                    last = nc.tensor.matmul(s.ps[:, 5, i * 8:i * 8 + 8], wT[:, o, i * P:(i + 1) * P], att[:, o, :], start=(o == 0), stop=(o == 1))
            last.then_inc(q["prep_mm"], 1)
            pe.wait_ge(q["prep_ok"], 1)
            transpose, multiply = pe_tile(pe)
            if layer == 1:
                run_ahead(pe, BLOCKS, transpose, multiply)
            else:
                run_tiles(pe, BLOCKS, 2, lambda k, u: (transpose(k, u), multiply(k, u)))

        @block.vector
        def _(dve):
            v = nc.vector
            step = Chain(dve, q["dve_step"])
            v.memset(s.wk[:, 528:544], 0.0).then_inc(q["att_z"], 1)
            step(v.memset(hrow, 1.0))
            dve.wait_ge(q["prep_t"], 1)
            v.tensor_copy(wT.rearrange("p i o -> p (i o)"), s.ps[:, 4, :]).then_inc(q["prep_sb"], 1)
            dve.wait_ge(q["prep_mm"], 1)
            v.tensor_copy(w[:, :, FEAT:FEAT + 8], s.ps[:, 5, 0:16].rearrange("p (h f) -> p h f", h=2)).then_inc(q["prep_ok"], 1)
            if layer == 2:
                dve.wait_ge(q["bias_ok"], 16)
            count, per = s.sem("agg_step"), 4

            def before_elu(k, u):
                if not peeled(k, 2):
                    dve.wait_ge(q["t_ok"], k - 1)
                n = [0]

                def steps(ins):
                    n[0] += 1
                    ins.then_inc(count, 1)
                    dve.wait_ge(count, k * per + n[0])
                row = hc[:, u, :]
                aggregate(nc, s, k, row, rec, steps)
                v.tensor_scalar(neg[:, u, :], row, 0.0, None, ALU.min).then_inc(q["neg_ok"], 1)
                v.tensor_scalar(row, row, 0.0, None, ALU.max).then_inc(count, 1)

            def elu(k, u):
                dve.wait_ge(count, k * per + per)
                dve.wait_ge(q["exp_ok"], k + 1)
                v.scalar_tensor_tensor(hc[:, u, :], neg[:, u, :], -1.0, hc[:, u, :], ALU.add, ALU.add).then_inc(q["in_ok"], 1)

            def evacuate(k, u):
                dve.wait_ge(q["mm_ok"], k + 1)
                if not peeled(k, 2):
                    dve.wait_ge(stored[u], (k - u) * 8)
                ps = s.ps[:, 2 + u, :]
                v.tensor_copy(hrow[:, u, :].rearrange("p (h f) -> p h f", h=HEADS)[:, :, 0:HID],
                              ps[:, 0:FEAT].rearrange("p (h f) -> p h f", h=HEADS)).then_inc(q["one_ok"], 1)
                v.tensor_copy(s.asd[:, bass.ds(k, 1), :].rearrange("p o h -> p (o h)"), ps[:, FEAT:FEAT + 8]).then_inc(q["mm_used"], 1)

            if layer == 1:
                run_ahead(dve, BLOCKS, lambda k, u: copy_t(dve, k, u), evacuate)
            else:
                def tile(k, u):
                    if not (isinstance(k, int) and k == 0):
                        evacuate(k - 1, 1 - u)
                    copy_t(dve, k, u)
                    before_elu(k + 1, 1 - u)
                    elu(k + 1, 1 - u)
                before_elu(0, 0)
                elu(0, 0)
                run_tiles(dve, BLOCKS - 1, 2, tile)
                evacuate(BLOCKS - 2, (BLOCKS - 2) % 2)
                copy_t(dve, BLOCKS - 1, (BLOCKS - 1) % 2)
                evacuate(BLOCKS - 1, (BLOCKS - 1) % 2)


def gat_scores(nc, s):
    idx_ok, batch_ok, dv, z_ok = (s.sem(n) for n in ("idx_ok", "batch_ok", "dve_step", "zeroed"))
    BATCH = 32
    batches = GATHERED // BATCH
    groups = (-(-TILES // BATCH) * BATCH - GATHERED) // LOOKED_UP
    assert batches % 2 == 0 and groups > 3
    got = s.swdge("got_scores", 2, [batches // 2 * BATCH * 16] * 2)
    base = s.sums
    by_edge = base[:, 0:ROWS * 4].rearrange("p (t h) -> p t h", h=4)
    inter = base[:, 0:ROWS * 4].rearrange("p (e h) -> p e h", h=4)
    seg = s.edge_x[:, :, 0:ROWS]
    ring_flat = s.ring[:, :, :].rearrange("p r f -> p (r f)")
    places = ([base[:, ROWS * 4 + c * 1024:ROWS * 4 + (c + 1) * 1024] for c in range(3)]
              + [s.wk[:, c * 1024:(c + 1) * 1024] for c in range(2)] + [ring_flat[:, c * 1024:(c + 1) * 1024] for c in range(2)])
    assert CHUNKS == len(places)
    first8 = [x.rearrange("p (e q) -> p e q", q=8) for x in places]
    until = s.w8[:, 0:ROWS]
    score = base[:, ROWS * 8:ROWS * 12].rearrange("p (h e) -> p h e", h=4)
    fill = base[:, ROWS * 12:ROWS * 13]
    npost = base[:, ROWS * 13:ROWS * 14]
    o = ROWS * 4
    hi_t = base[:, o:o + ROWS]
    picked = base[:, o + ROWS:o + ROWS + 2 * LOOKED_UP * 4 * BLOCKS].rearrange("p (u n) -> p u n", u=2)
    hi_i = picked[:, 0, 0:ROWS].bitcast(I32)
    o += ROWS + 2 * LOOKED_UP * 4 * BLOCKS
    mask = base[:, o:o + 2 * LOOKED_UP * BLOCKS].rearrange("p (u t n) -> p u t n", u=2, n=BLOCKS)
    o += 2 * LOOKED_UP * BLOCKS
    parts = base[:, o:o + 6 * BLOCKS].bitcast(BF16).rearrange("p (q n) -> p q n", q=3)
    p_f = base[:, o + 6 * BLOCKS:o + 6 * BLOCKS + 1]
    rest, wide_part = picked[:, 1, 0:4 * BLOCKS], picked[:, 1, 4 * BLOCKS:8 * BLOCKS]
    lo_bc = s.work[:, 2048:4096].bitcast(BF16).rearrange("p (u e) -> p u e", u=2)
    hot = ring_flat[:, 0:2048].bitcast(BF16).rearrange("p (u e) -> p u e", u=2)
    hot_ok, table_ok, row_in, mask_ok, pick_ok, sum_ok = (s.sem(n) for n in
        ("hot_ok", "table_ok", "row_in", "mask_ok", "pick_ok", "sum_ok"))
    lo_in = [s.sem("lo_in") for _ in range(2)]
    by_slot = base[:, 0:SLOT_CHUNKS * 512].rearrange("p (c e) -> p c e", e=512)
    stage = s.work[:, 0:2 * BATCH].bitcast(I32).rearrange("p (u n) -> p u n", u=2)
    ringa = s.work[:, 64:64 + 2 * BATCH * 4].rearrange("p (u n) -> p u n", u=2)
    amax = s.work[:, 512:512 + BLOCKS * 4].rearrange("p (k h) -> p k h", h=4)
    t4 = s.work[:, 768:768 + BLOCKS * 4].rearrange("p (k h) -> p k h", h=4)
    lasts = s.work[:, 1024:1024 + CHUNKS * 8].rearrange("p (c q) -> p c q", q=8)
    carry = s.work[:, 1088:1088 + CHUNKS * 8].rearrange("p (c q) -> p c q", q=8)
    line = s.work[0:8, 1152:1152 + ROWS + 1]
    line_in = s.work[0:8, 2560:2560 + ROWS]
    tr_ok, row_ok, last_ok, lineT, line_ok, carry_t = (s.sem(n) for n in
        ("tr_ok", "row_ok", "last_ok", "line_t", "line_ok", "carry_t"))
    max_made, max_st, node_ok, self_ok, got_first = (s.sem(n) for n in
        ("max_made", "max_stored", "node_ok", "self_ok", "got_first"))
    z4_ok, e_ok, ex_st, ext, exs = (s.sem(n) for n in ("z4_ok", "e_ok", "ex_stored", "ex_t", "ex_s"))
    (got_max, max0), = s.swdge("got_max", 1, [16 * BLOCKS])
    (sc_st, sc0), = s.swdge("scattered", 1, [16 * BLOCKS])
    (got_ex, ex0), = s.swdge("got_ex", 1, [16 * SLOT_CHUNKS])
    ps = s.ps

    with nc.Block() as block:
        @block.gpsimd
        def _(pool):
            for k in range(BLOCKS):
                pool.indirect_dma_start(out=s.fill_rows, out_offset=bass.IndirectOffsetOnAxis(ap=s.first_i[:, k:k + 1], axis=0),
                                        in_=s.asd[:, k, :], in_offset=None,
                                        bounds_check=ROWS * P - 1, oob_is_err=False).then_inc(sc_st, 16)

            def batch(g, u):
                pool_wait(pool, s, idx_ok, g + 1)
                if not peeled(g, 2):
                    pool_wait(pool, s, batch_ok, g - 1)
                for n in range(BATCH):
                    pool.indirect_dma_start(out=ringa[:, u, 4 * n:4 * n + 4], out_offset=None, in_=s.as_rows,
                                            in_offset=bass.IndirectOffsetOnAxis(ap=stage[:, u, n:n + 1], axis=0)).then_inc(got[u][0], 16)
            run_tiles(pool, batches, 2, batch)
            pool.wait_ge(max_st, 16 * CHUNKS)
            for k in range(BLOCKS):
                pool.indirect_dma_start(out=amax[:, k, :], out_offset=None, in_=s.max_rows,
                                        in_offset=bass.IndirectOffsetOnAxis(ap=s.last_i[:, k:k + 1], axis=0)).then_inc(got_max, 16)
            pool.wait_ge(ex_st, 16 * CHUNKS)
            for c in range(SLOT_CHUNKS):
                pool.indirect_dma_start(out=by_slot[:, c, :], out_offset=None, in_=s.ex_rows,
                                        in_offset=bass.IndirectOffsetOnAxis(ap=s.t_slot[:, c:c + 1], axis=0)).then_inc(got_ex, 16)

        @block.sync
        def _(sp):
            lines = s.lo_rows.rearrange("(t k) e -> t (k e)", k=LOOKED_UP)

            def load(j, u):
                if not peeled(j, 2):
                    sp.wait_ge(hot_ok, j - 1)
                sp.dma_start(lo_bc[:, u, :], lines[bass.ds(GATHERED // LOOKED_UP + j, 1), :].broadcast_to([P, LOOKED_UP * P])).then_inc(lo_in[u], 16)
            run_tiles(sp, groups, 2, load)
            sp.wait_ge(sc_st, 16 * BLOCKS + sc0)
            sp.wait_ge(sum_ok, groups)
            rows = s.fill_rows.rearrange("(c p e) q -> c p (e q)", p=P, e=P)
            for c in range(CHUNKS):
                sp.dma_start(places[c], rows[c]).then_inc(got_first, 16)
            sp.wait_ge(max_made, 1)
            rows = s.max_rows.rearrange("(c p e) h -> c p (e h)", p=P, e=P)
            for c in range(CHUNKS):
                sp.dma_start(rows[c], inter[:, c * P:(c + 1) * P, :].rearrange("p e h -> p (e h)")).then_inc(max_st, 16)
            sp.wait_ge(e_ok, HEADS)
            rows = s.ex_rows.rearrange("(c p) (h e) -> c p h e", p=P, e=P)
            for c in range(CHUNKS):
                sp.dma_start(rows[c], score[:, :, c * P:(c + 1) * P]).then_inc(ex_st, 16)
            sp.wait_ge(ex_st, 16 * CHUNKS)

        @block.scalar
        def _(act):
            def put(g, u):
                if not peeled(g, 2):
                    act.wait_ge(batch_ok, g - 1)
                nc.scalar.activation(stage[:, u, :], s.src_t[:, bass.ds(g * BATCH, BATCH)], ACT.Copy).then_inc(idx_ok, 1)

            def take(g, u):
                act.wait_ge(got[u][0], ((g - u) * 8 + 16) * BATCH + got[u][1])
                nc.scalar.activation(by_edge[:, bass.ds(g * BATCH, BATCH), :].rearrange("p t h -> p (t h)"), ringa[:, u, :], ACT.Copy).then_inc(batch_ok, 1)
            for u in range(2):
                put(u, u)
            take(0, 0)

            put(2, 0)
            take(1, 1)
            put(3, 1)
            with act.Fori(1, batches // 2 - 1) as i:
                for u in range(2):
                    take(i * 2 + u, u)
                    put(i * 2 + u + 2, u)
            for g in range(batches // 2 * 2 - 2, batches):
                take(g, g % 2)
            act.wait_ge(z_ok, 1)
            for c in range(CHUNKS):
                act.wait_ge(tr_ok, c + 1)
                nc.scalar.activation(score[:, :, c * P:(c + 1) * P], ps[:, c % 2, :].rearrange("p (h e) -> p h e", h=4), ACT.Copy).then_inc(row_ok, 1)
            for h in range(HEADS):
                act.wait_ge(z4_ok, h + 1)
                nc.scalar.activation(score[:, h, :], score[:, h, :], ACT.Exp).then_inc(e_ok, 1)
            act.wait_ge(node_ok, 1)
            nc.scalar.activation(s.exself[:, :, :], s.exself[:, :, :], ACT.Exp).then_inc(self_ok, 1)
            for c in range(SLOT_CHUNKS):
                act.wait_ge(ext, c + 1)
                nc.scalar.activation(s.edge_x[:, :, c * P:(c + 1) * P], ps[:, 6 + c % 2, :].rearrange("p (h e) -> p h e", h=4), ACT.Copy).then_inc(exs, 1)

        @block.tensor
        def _(pe):
            t = nc.tensor
            pe.wait_ge(table_ok, 1)

            def look_up(j, u):
                pe.wait_ge(hot_ok, j + 1)
                for i in range(LOOKED_UP // 2):
                    n = j * (LOOKED_UP // 2) + i
                    if not (isinstance(j, int) and n < 8):
                        pe.wait_ge(pick_ok, n - 7)
                    for k in range(2):
                        e = (2 * i + k) * P
                        for q in range(3):
                            last = t.matmul(ps[:, i, k * 4 * BLOCKS:(k + 1) * 4 * BLOCKS], hot[:, u, e:e + P], parts[:, q, :],
                                            start=(k == 0 and q == 0), stop=(k == 1 and q == 2), skip_group_check=True)
                    last.then_inc(row_in, 1)
            run_tiles(pe, groups, 2, look_up)
            pe.wait_ge(sum_ok, groups)
            pe.wait_ge(batch_ok, batches)
            pe.wait_ge(z_ok, 1)
            for c in range(CHUNKS):
                if c >= 2:
                    pe.wait_ge(row_ok, c - 1)
                for h in range(HEADS):
                    last = t.transpose(ps[:, c % 2, h * P:(h + 1) * P], by_edge[:, c * P:(c + 1) * P, h], s.ident[:, :])
                last.then_inc(tr_ok, 1)
            for n, w, shift in ((1, 4, 0), (2, 8, 0), (3, 4, 1)):
                pe.wait_ge(last_ok, n)
                for c in range(CHUNKS):
                    last = t.transpose(ps[0:w, 2 + c // 4, c % 4 * P:c % 4 * P + P], lasts[:, c, 0:w], s.ident[:, :])
                last.then_inc(lineT, 1)
                pe.wait_ge(line_ok, n)
                for c in range(CHUNKS):
                    last = t.transpose(ps[:, 4, c * 8:c * 8 + w], line[0:w, c * P + shift:(c + 1) * P + shift], s.ident[0:w, 0:w])
                last.then_inc(carry_t, 1)
            for c in range(SLOT_CHUNKS):
                pe.wait_ge(got_ex, 16 * SLOT_CHUNKS + ex0)
                if c >= 2:
                    pe.wait_ge(exs, c - 1)
                for h in range(HEADS):
                    last = t.transpose(ps[:, 6 + c % 2, h * P:(h + 1) * P], by_slot[:, c, h * P:(h + 1) * P], s.ident[:, :])
                last.then_inc(ext, 1)

        @block.vector
        def _(dve):
            v = nc.vector
            step = Chain(dve, dv)
            v.memset(by_edge[:, GATHERED + groups * LOOKED_UP:ROWS, :], 0.0).then_inc(z_ok, 1)
            step(v.tensor_copy(rest.rearrange("p (h k) -> p h k", h=4), s.asd[:, :, 0:4].rearrange("p k h -> p h k")))
            for q in range(3):
                step(v.tensor_copy(parts[:, q, :], rest))
                if q < 2:
                    step(v.tensor_copy(wide_part, parts[:, q, :]))
                    step(v.tensor_tensor(rest, rest, wide_part, ALU.subtract))
            step(v.tensor_scalar(hi_i, s.src_t[:, :], 7, None, ALU.logical_shift_right))
            step(v.tensor_copy(hi_t, hi_i))
            step(v.tensor_tensor(wide_part[:, 0:P], s.ident[:, :], s.iota[:, :], ALU.mult))
            v.tensor_reduce(p_f, wide_part[:, 0:P], AX.X, ALU.add).then_inc(table_ok, 1)
            dve.wait_ge(table_ok, 1)

            def one_hot(j, u):
                dve.wait_ge(lo_in[u], (j - u) * 8 + 16)
                if not peeled(j, 2):
                    dve.wait_ge(row_in, (j - 1) * (LOOKED_UP // 2))
                v.tensor_scalar(hot[:, u, :], lo_bc[:, u, :], p_f, None, ALU.is_equal).then_inc(hot_ok, 1)

            def add_up(j, u):
                dve.wait_ge(pick_ok, (j + 1) * (LOOKED_UP // 2))
                v.tensor_reduce(by_edge[:, bass.ds(GATHERED + j * LOOKED_UP, LOOKED_UP), :].rearrange("p t h -> p (t h)"),
                                picked[:, u, :].rearrange("p (t k) -> p t k", k=BLOCKS), AX.X, ALU.add).then_inc(sum_ok, 1)

            def pick(j, u, final=False):
                hi = hi_t[:, bass.ds(GATHERED + j * LOOKED_UP, LOOKED_UP)]
                v.tensor_tensor(mask[:, u, :, :], s.iota[:, 0:BLOCKS].unsqueeze(1).broadcast_to([P, LOOKED_UP, BLOCKS]),
                                hi.unsqueeze(2).broadcast_to([P, LOOKED_UP, BLOCKS]), ALU.is_equal).then_inc(mask_ok, 1)
                if not final:
                    one_hot(j + 1, 1 - u)
                if not (isinstance(j, int) and j == 0):
                    add_up(j - 1, 1 - u)
                dve.wait_ge(mask_ok, j + 1)
                if not peeled(j, 2):
                    dve.wait_ge(sum_ok, j - 1)
                for i in range(LOOKED_UP // 2):
                    dve.wait_ge(row_in, j * (LOOKED_UP // 2) + i + 1)
                    m = mask[:, u, 2 * i:2 * i + 2, :].unsqueeze(2).broadcast_to([P, 2, 4, BLOCKS])
                    v.tensor_tensor(picked[:, u, i * 8 * BLOCKS:(i + 1) * 8 * BLOCKS].rearrange("p (t h k) -> p t h k", t=2, h=4),
                                    ps[:, i, 0:8 * BLOCKS].rearrange("p (t h k) -> p t h k", t=2, h=4), m, ALU.mult).then_inc(pick_ok, 1)
            one_hot(0, 0)
            run_tiles(dve, groups - 1, 2, pick)
            pick(groups - 1, (groups - 1) % 2, True)
            add_up(groups - 1, (groups - 1) % 2)
            until3, keep3, fill3 = (x.rearrange("p (c e) -> p c e", e=P) for x in (until, s.keep[:, :], fill))
            dve.wait_ge(sum_ok, groups)
            step(v.memset(until3[:, :, P - 1:P], 0.0))
            step(v.tensor_copy(until3[:, :, 0:P - 1], keep3[:, :, 1:P]))
            step(v.memset(fill, 0.0))
            step(v.memset(fill3[:, :, P - 1:P], 1.0))
            step(v.tensor_tensor_scan(npost[:, ::-1], until[:, ::-1], fill[:, ::-1], 0.0, ALU.mult, ALU.add))
            step(v.tensor_scalar(npost, npost, -1.0, BIG, ALU.add, ALU.mult))
            step(v.tensor_scalar(until, until, -1.0, BIG, ALU.add, ALU.mult))
            dve.wait_ge(row_ok, CHUNKS)
            for h in range(HEADS):
                last = v.tensor_tensor_scan(seg[:, h, :], s.dmax[:, :], score[:, h, :], -BIG, ALU.add, ALU.max)
            step(last)

            def carries(n, w, keep, initial, op0, op1, back=False):
                dve.wait_ge(lineT, n)
                step(v.tensor_copy(line_in[0:w, 0:512], ps[0:w, 2, :]))
                step(v.tensor_copy(line_in[0:w, 512:ROWS], ps[0:w, 3, 0:ROWS - 512]))
                if back:
                    step(v.memset(line[0:w, ROWS:ROWS + 1], initial))
                    v.tensor_tensor_scan(line[0:w, 0:ROWS][:, ::-1], keep[0:w, ::-1], line_in[0:w, ::-1], initial, op0, op1).then_inc(line_ok, 1)
                else:
                    step(v.memset(line[0:w, 0:1], initial))
                    v.tensor_tensor_scan(line[0:w, 1:ROWS + 1], keep[0:w, :], line_in[0:w, :], initial, op0, op1).then_inc(line_ok, 1)
                dve.wait_ge(carry_t, n)
                step(v.tensor_copy(carry[:, :, 0:w], ps[:, 4, 0:CHUNKS * 8].rearrange("p (c q) -> p c q", q=8)[:, :, 0:w]))

            seg4 = seg.rearrange("p h (c e) -> p c h e", e=P)
            v.tensor_copy(lasts[:, :, 0:4], seg4[:, :, :, P - 1]).then_inc(last_ok, 1)
            carries(1, 4, s.dmax_r, -BIG, ALU.add, ALU.max)
            for c in range(CHUNKS):
                for h in range(HEADS):
                    part = slice(c * P, (c + 1) * P)
                    last = v.scalar_tensor_tensor(inter[:, part, h], s.npre[:, part], carry[:, c, h:h + 1], seg[:, h, part], ALU.add, ALU.max)
            last.then_inc(max_made, 1)
            dve.wait_ge(got_first, 16 * CHUNKS)
            for c in range(CHUNKS):
                for n in range(8):
                    last = v.tensor_tensor_scan(first8[c][:, :, n], s.keep[:, c * P:(c + 1) * P], first8[c][:, :, n], 0.0, ALU.mult, ALU.add)
            step(last)
            for c in range(CHUNKS):
                last = v.tensor_copy(lasts[:, c, :], first8[c][:, P - 1, :])
            last.then_inc(last_ok, 1)
            dve.wait_ge(max_made, 1)
            for h in range(HEADS):
                last = v.tensor_tensor_scan(seg[:, h, ::-1], until[:, ::-1], inter[:, ::-1, h], -BIG, ALU.add, ALU.max)
            step(last)
            carries(2, 8, s.keep_r, 0.0, ALU.mult, ALU.add)
            for c in range(CHUNKS):
                for n in range(8):
                    last = v.scalar_tensor_tensor(first8[c][:, :, n], s.pre[:, c * P:(c + 1) * P], carry[:, c, n:n + 1],
                                                  first8[c][:, :, n], ALU.mult, ALU.add)
            step(last)
            v.tensor_tensor(lasts[:, :, 0:4], seg4[:, :, :, 0], s.n0[:, :].unsqueeze(2).broadcast_to([P, CHUNKS, 4]), ALU.add).then_inc(last_ok, 1)
            carries(3, 4, s.dmax_r, -BIG, ALU.add, ALU.max, back=True)
            for h in range(HEADS):
                for c in range(CHUNKS):
                    part = slice(c * P, (c + 1) * P)
                    last = v.scalar_tensor_tensor(seg[:, h, part], npost[:, part], carry[:, c, h:h + 1], seg[:, h, part], ALU.add, ALU.max)
                step(last)
                for c in range(CHUNKS):
                    part = slice(c * P, (c + 1) * P)
                    last = v.tensor_tensor(seg[:, h, part], seg[:, h, part], first8[c][:, :, h], ALU.max)
                step(last)
                for c in range(CHUNKS):
                    part = slice(c * P, (c + 1) * P)
                    v.tensor_tensor(score[:, h, part], score[:, h, part], first8[c][:, :, h + 4], ALU.add)
                    last = v.tensor_tensor(seg[:, h, part], seg[:, h, part], first8[c][:, :, h + 4], ALU.add)
                step(last)
                step(v.scalar_tensor_tensor(fill, score[:, h, :], 0.2, score[:, h, :], ALU.mult, ALU.max))
                step(v.scalar_tensor_tensor(seg[:, h, :], seg[:, h, :], 0.2, seg[:, h, :], ALU.mult, ALU.max))
                step(v.tensor_tensor(fill, fill, seg[:, h, :], ALU.subtract))
                v.tensor_scalar(score[:, h, :], fill, 0.0, None, ALU.min).then_inc(z4_ok, 1)
                if h < HEADS - 1:
                    dve.wait_ge(z4_ok, h + 1)
            dve.wait_ge(got_max, 16 * BLOCKS + max0)
            a_s, a_d = s.asd[:, :, 0:4], s.asd[:, :, 4:8]
            wide = lambda t: t[:, :].unsqueeze(2).broadcast_to([P, BLOCKS, 4])
            step(v.tensor_tensor(amax, amax, wide(s.has), ALU.mult))
            step(v.tensor_tensor(amax, amax, wide(s.hasb), ALU.add))
            step(v.tensor_tensor(amax, amax, a_s, ALU.max))
            step(v.tensor_tensor(amax, amax, a_d, ALU.add))
            step(v.scalar_tensor_tensor(amax, amax, 0.2, amax, ALU.mult, ALU.max))
            step(v.tensor_tensor(t4, a_s, a_d, ALU.add))
            step(v.scalar_tensor_tensor(t4, t4, 0.2, t4, ALU.mult, ALU.max))
            v.tensor_tensor(s.exself[:, :, :], t4, amax, ALU.subtract).then_inc(node_ok, 1)


def gat_edges(nc, s):
    idx_ok, msg_ok, sel_ok, agg_ok, own_ok, z_ok = (s.sem(n) for n in
        ("idx_ok", "msg_ok", "sel_ok", "agg_ok", "own_ok", "z_ok"))
    got = s.swdge("ring", RING, [SLOTS // RING * 16] * RING)
    cuts = [(0, 8), (8, 28), (28, BLOCKS)]
    own_in = [s.sem("own_in") for _ in cuts]
    msg = s.work[:, 0:4 * ROW].rearrange("p (b k f) -> p b k f", b=2, k=2)
    sel = s.work[:, 2048:2048 + 4 * P].rearrange("p (b k n) -> p b k n", b=2, k=2)
    with nc.Block() as block:
        @block.sync
        def _(sp):
            for n, (lo, hi) in enumerate(cuts):
                sp.dma_start(s.sums[:, lo * ROW:hi * ROW].rearrange("p (k f) -> p k f", f=ROW),
                             s.h_rows[lo * P:hi * P, :].rearrange("(k p) f -> p k f", p=P)).then_inc(own_in[n], 16)

        @block.gpsimd
        def _(pool):
            gather_slots(pool, s, s.h_rows, ROW, idx_ok, got, msg_ok)

        @block.scalar
        def _(act):
            def stage(g, u):
                if not peeled(g, 2):
                    act.wait_ge(msg_ok, (g - 1) * 8)
                nc.scalar.activation(s.idx[:, u, :], s.src_x[:, bass.ds(g * GROUP, GROUP)], ACT.Copy).then_inc(idx_ok, 1)
            run_tiles(act, GROUPS, 2, stage)

        @block.tensor
        def _(pe):
            def collect(g, q):
                pair, b = g * 8 + q, q % 2
                pe.wait_ge(msg_ok, pair + 1)
                pe.wait_ge(sel_ok, pair + 1)
                if not (isinstance(g, int) and g == 0 and q < 2):
                    pe.wait_ge(z_ok, pair - 1)
                for k in range(2):
                    last = nc.tensor.matmul(s.ps[:, b, 0:ROW], sel[:, b, k, :], msg[:, b, k, :], start=(k == 0), stop=(k == 1))
                last.then_inc(agg_ok, 1)

            def group(g, u):
                for q in range(8):
                    collect(g, q)
            run_tiles(pe, GROUPS, 2, group)

        @block.vector
        def _(dve):
            v = nc.vector

            def own(n):
                lo, hi = cuts[n]
                dve.wait_ge(own_in[n], 16)
                rows = s.sums[:, lo * ROW:hi * ROW].rearrange("p (q f) -> p q f", f=HID + 1)
                ex = s.exself[:, lo:hi, :].rearrange("p k h -> p (k h)").unsqueeze(2).broadcast_to([P, (hi - lo) * HEADS, HID + 1])
                v.tensor_tensor(rows, rows, ex, ALU.mult).then_inc(own_ok, 1)

            def make(g, q):
                pair, b = g * 8 + q, q % 2
                if not (isinstance(g, int) and g == 0 and q < 2):
                    dve.wait_ge(agg_ok, pair - 1)
                for k in range(2):
                    last = v.tensor_scalar(sel[:, b, k, :], s.iota[:, :], s.dst_x[:, bass.ds(pair * 2 + k, 1)], None, ALU.is_equal)
                last.then_inc(sel_ok, 1)
                landed(dve, got, g, 2 * q)
                landed(dve, got, g, 2 * q + 1)
                r = 2 * q % RING
                ex = s.edge_x[:, :, bass.ds(pair * 2, 2)].rearrange("p h k -> p k h").unsqueeze(3).broadcast_to([P, 2, HEADS, HID + 1])
                v.tensor_tensor(msg[:, b, :, :].rearrange("p k (h f) -> p k h f", h=HEADS),
                                s.ring[:, r:r + 2, :].rearrange("p k (h f) -> p k h f", h=HEADS), ex, ALU.mult).then_inc(msg_ok, 1)

            add8 = adder(nc, s, dve, s.sums, agg_ok, z_ok, ROW, lambda b: s.ps[:, b, 0:ROW])

            def group(g, u):
                for q in range(8):
                    n = {(0, 0): 0, (1, 0): 1, (1, 7): 2}.get((g, q)) if isinstance(g, int) else None
                    if n is not None:
                        own(n)
                    make(g, q)
                    if n is not None:
                        dve.wait_ge(own_ok, n + 1)
                    if isinstance(g, int) and g == 0 and q == 0:
                        continue
                    if q:
                        add8(g, (q - 1) // 2, (q - 1) % 2)
                    else:
                        add8(g - 1, 3, 1)
            run_tiles(dve, GROUPS, 2, group)
            add8(GROUPS - 1, 3, 1)


def gat_out(nc, s, a, out):
    bias_ok, neg_ok, exp_ok, count, out_ok = (s.sem(n) for n in ("bias_ok", "neg_ok", "exp_ok", "agg_step", "out_ok"))
    stored = [s.sem("stored") for _ in range(4)]
    wk = s.work
    row = wk[:, 0:1024].rearrange("p (u f) -> p u f", u=4)
    neg = wk[:, 1024:2048].rearrange("p (u f) -> p u f", u=4)
    rec = wk[:, 2308:2312]
    with nc.Block() as block:
        @block.sync
        def _(sp):
            sp.dma_start(s.bias[:, 0, :], a["b2"].rearrange("(o n) -> o n", o=1).broadcast_to([P, FEAT])).then_inc(bias_ok, 16)

        @block.scalar
        def _(act):
            def negative(k, u):
                act.wait_ge(neg_ok, k + 1)
                nc.scalar.activation(neg[:, u, :], neg[:, u, :], ACT.Exp).then_inc(exp_ok, 1)

            def store(k, u):
                act.wait_ge(out_ok, k + 1)
                n = min(P, NODES - k * P) if isinstance(k, int) else P
                act.dma_start(out[bass.ds(k * P, n), :], row[0:n, u, :]).then_inc(stored[u], 16)
            run_ahead(act, BLOCKS, negative, store, 4)
            for u in range(4):
                act.wait_ge(stored[u], 16 * ((BLOCKS + 3 - u) // 4))

        @block.vector
        def _(dve):
            v = nc.vector
            dve.wait_ge(bias_ok, 16)
            per = 4

            def before_elu(k, u):
                if not peeled(k, 4):
                    dve.wait_ge(stored[u], (k - u) * 4)
                n = [0]

                def steps(ins):
                    n[0] += 1
                    ins.then_inc(count, 1)
                    dve.wait_ge(count, k * per + n[0])
                r = row[:, u, :]
                aggregate(nc, s, k, r, rec, steps)
                v.tensor_scalar(neg[:, u, :], r, 0.0, None, ALU.min).then_inc(neg_ok, 1)
                v.scalar_tensor_tensor(r, r, 0.0, s.xr[:, bass.ds(k, 1), :].rearrange("p o f -> p (o f)"), ALU.max, ALU.add).then_inc(count, 1)

            def elu(k, u):
                dve.wait_ge(count, k * per + per)
                dve.wait_ge(exp_ok, k + 1)
                v.scalar_tensor_tensor(row[:, u, :], neg[:, u, :], -1.0, row[:, u, :], ALU.add, ALU.add).then_inc(out_ok, 1)
            run_ahead(dve, BLOCKS, before_elu, elu, 4)


def kernel(**inputs):
    import numpy as np
    import concourse.bacc as bacc
    from concourse.bass_utils import run_bass_kernel_spmd

    def get(name):
        return np.ascontiguousarray(inputs[name])

    def rows(x, count, fill):
        x = np.asarray(x)
        full = np.full((count,) + x.shape[1:], fill, x.dtype)
        full[:x.shape[0]] = x
        return full

    none = BLOCKS * P
    dst = rows(get("dst"), ROWS * P, none)
    src = rows(get("src"), ROWS * P, 0)
    prev = np.concatenate([np.full(1, -1, dst.dtype), dst[:-1]])
    ea4 = rows(get("edge_attr_4"), ROWS * P, 0).reshape(ROWS, P, 4)
    ea8 = rows(get("edge_attr_8"), ROWS * P, 0).reshape(ROWS, P, 8)
    arrays = {
        "x": rows(get("x"), BLOCKS * P, 0),
        "a_cols": rows(get("node_vec1"), BLOCKS * P, 0).reshape(BLOCKS, P).T,
        "dst_rows": dst.reshape(ROWS, P),
        "prev_rows": prev.reshape(ROWS, P),
        "src_t": src.reshape(ROWS, P).T,
        "sd_rows": np.concatenate([src.reshape(ROWS, P), dst.reshape(ROWS, P)], 1),
        "ea4_rows": ea4.transpose(0, 2, 1).reshape(ROWS, 4 * P),
        "ea8_rows": ea8.transpose(0, 2, 1).reshape(ROWS * 8, P),
    }
    for n in ("sc_w0", "sc_w1", "lin1_w0", "lin1_w1", "fc_w1", "fc_w2", "lin2_w00", "lin2_w01", "lin2_w10", "lin2_w11"):
        arrays[n] = get("L0_gnn_" + n)
    for n in ("W1", "att_src1", "att_dst1", "b1", "W2", "att_src2", "att_dst2", "b2"):
        arrays[n] = get("L1_gnn_" + n)
    arrays = {n: np.ascontiguousarray(v) for n, v in arrays.items()}
    nc = bacc.Bacc("TRN2", target_bir_lowering=False, num_devices=1)
    a = {n: nc.dram_tensor("in_" + n, v.shape, mybir.dt.from_np(v.dtype), kind="ExternalInput").ap() for n, v in arrays.items()}
    out = nc.dram_tensor("out", (NODES, FEAT), F32, kind="ExternalOutput").ap()
    build(nc, a, out)
    result = run_bass_kernel_spmd(nc, [{"in_" + n: v for n, v in arrays.items()}], core_ids=[0])
    return result.results[0]["out"]
```
